# Optimizing a Trainium2 kernel written in Bass

```python
import numpy as np
import jax
import jax.numpy as jnp

def _softmax(x, axis=-1):
    return jax.nn.softmax(x, axis=axis)

def _gelu(x):
    return jax.nn.gelu(x, approximate=True)

def _silu(x):
    return jax.nn.silu(x)

def _sigmoid(x):
    return jax.nn.sigmoid(x)

def _layernorm(x, axis=-1, eps=1e-05):
    m = jnp.mean(x, axis=axis, keepdims=True)
    v = jnp.var(x, axis=axis, keepdims=True)
    return (x - m) / jnp.sqrt(v + eps)

def _scatter_add(tgt, idx, src, axis=0):
    return tgt.at[idx].add(src)

def _segment_sum(src, seg, n):
    return jax.ops.segment_sum(src, seg, n)
kernel_name = 'mk_gnn_resnorm_d4_gnn_r32_04b5f3'

def setup_inputs(seed: int=0):
    np.random.seed(seed)
    _w = jnp.asarray

    def _rec_inputs():
        import jax
        import jax.numpy as jnp
        _gk = jax.random.key(seed)
        x = -0.0001978 + 0.9998 * jax.random.normal(jax.random.fold_in(_gk, 1), (3125, 128), jnp.float32)
        src = jax.random.randint(jax.random.fold_in(_gk, 2), (100000,), 0, 3125, jnp.int32)
        dst = jnp.minimum((3125 * jax.random.uniform(jax.random.fold_in(_gk, 3), (100000,)) ** 2.0).astype(jnp.int32), 99999)
        _o = jnp.argsort(dst, stable=True)
        src = src[_o]
        dst = dst[_o]
        edge_weight = jax.random.uniform(jax.random.fold_in(_gk, 13), (100000,), jnp.float32, 0.0, 0.0625)
        edge_weight1 = 0.00171547 + 0.999346 * jax.random.normal(jax.random.fold_in(_gk, 14), (100000, 1), jnp.float32)
        return (x, src, dst, edge_weight, edge_weight1)
    x, src, dst, edge_weight, edge_weight1 = _rec_inputs()

    def _L0_gnn_setup():
        import jax, jax.numpy as jnp
        import numpy as np
        N, DIM, K = (50000, 128, 9)
        FFN = 4 * DIM
        EPS = 1e-05

        def layer_norm(x, g, b):
            mu = jnp.mean(x, axis=-1, keepdims=True)
            var = jnp.mean(jnp.square(x - mu), axis=-1, keepdims=True)
            return (x - mu) * jax.lax.rsqrt(var + EPS) * g + b
        key = jax.random.key(seed)
        ks = jax.random.split(key, 12)
        E = N * K
        src = jax.random.randint(ks[0], (E,), 0, N)
        dst = jnp.repeat(jnp.arange(N), K)
        edge_index = jnp.stack([src, dst]).astype(jnp.int64)
        s = lambda k, shape, fan_in: jax.random.normal(k, shape, jnp.float32) / np.sqrt(fan_in)
        return {'x': jax.random.normal(ks[1], (N, DIM), jnp.float32), 'edge_index': edge_index, 'W_in_w': s(ks[2], (DIM, DIM), DIM), 'W_in_b': jnp.zeros((DIM,), jnp.float32), 'W_upd_w': s(ks[3], (2 * DIM, DIM), 2 * DIM), 'W_upd_b': jnp.zeros((DIM,), jnp.float32), 'W_out_w': s(ks[4], (DIM, DIM), DIM), 'W_out_b': jnp.zeros((DIM,), jnp.float32), 'ln1_g': jnp.ones((DIM,), jnp.float32), 'ln1_b': jnp.zeros((DIM,), jnp.float32), 'ln2_g': jnp.ones((DIM,), jnp.float32), 'ln2_b': jnp.zeros((DIM,), jnp.float32), 'ffn1_w': s(ks[5], (DIM, FFN), DIM), 'ffn1_b': jnp.zeros((FFN,), jnp.float32), 'ffn2_w': s(ks[6], (FFN, DIM), FFN), 'ffn2_b': jnp.zeros((DIM,), jnp.float32)}
    _L0_gnn_all = _L0_gnn_setup()
    _L0_gnn_in = {k: v for k, v in _L0_gnn_all.items() if k in ('W_in_w', 'W_in_b', 'W_upd_w', 'W_upd_b', 'W_out_w', 'W_out_b', 'ln1_g', 'ln1_b', 'ln2_g', 'ln2_b', 'ffn1_w', 'ffn1_b', 'ffn2_w', 'ffn2_b')}
    del _L0_gnn_all

    def _L1_gnn_setup():
        import jax, jax.numpy as jnp
        import numpy as np
        N = 3125
        E = 50000
        D = 128
        NEG_SLOPE = 0.2
        EPS = 1e-12
        key = jax.random.key(seed)
        k1, k2, k3, k4, k5, k6 = jax.random.split(key, 6)
        ego = jax.random.normal(k1, (N, D), dtype=jnp.float32)
        std = float(np.sqrt(2.0 / (D + D)))
        W1 = jax.random.normal(k2, (D, D), dtype=jnp.float32) * std
        W2 = jax.random.normal(k3, (D, D), dtype=jnp.float32) * std
        b1 = jnp.zeros((1, D), dtype=jnp.float32)
        b2 = jnp.zeros((1, D), dtype=jnp.float32)
        src = jax.random.randint(k4, (E,), 0, N)
        dst = jax.random.randint(k5, (E,), 0, N)
        adj_vals = jax.random.uniform(k6, (E,), dtype=jnp.float32) * (1.0 / 16.0)
        return {'ego_embeddings': ego, 'W1': W1, 'W2': W2, 'b1': b1, 'b2': b2, 'adj_vals': adj_vals, 'src': src, 'dst': dst}
    _L1_gnn_all = _L1_gnn_setup()
    _L1_gnn_in = {k: v for k, v in _L1_gnn_all.items() if k in ('W1', 'W2', 'b1', 'b2')}
    del _L1_gnn_all

    def _L2_gnn_setup():
        import jax, jax.numpy as jnp
        import numpy as np

        def _gat_layer(h, d, src, dst, W0_l, W1_l, W2_l, Wa_l, N):
            t = d @ W0_l
            z = h @ W1_l
            z_i = h @ W2_l
            z_src = z[src]
            z_dst = z[dst]
            e = jax.nn.leaky_relu(jnp.concatenate([z_src, z_dst, t], axis=1) @ Wa_l)[:, 0]
            m = jax.ops.segment_max(e, dst, num_segments=N)
            m = jnp.where(jnp.isfinite(m), m, 0.0)
            ex = jnp.exp(e - m[dst])
            denom = jax.ops.segment_sum(ex, dst, num_segments=N)
            alpha = ex / denom[dst]
            z_neighbor = jax.ops.segment_sum(z_src * alpha[:, None], dst, num_segments=N)
            return jax.nn.relu(z_i + z_neighbor)
        key = jax.random.key(seed)
        ks = jax.random.split(key, 8)
        N, E, D, L = (1250, 20000, 128, 3)
        attr = jax.random.normal(ks[0], (N, D), dtype=jnp.float32)
        d = jax.random.normal(ks[1], (E, 1), dtype=jnp.float32)
        src = jax.random.randint(ks[2], (E,), 0, N)
        dst = jax.random.randint(ks[3], (E,), 0, N)
        s = 1.0 / np.sqrt(D)
        W0 = jax.random.normal(ks[4], (L, 1, 1), dtype=jnp.float32)
        W1 = jax.random.normal(ks[5], (L, D, D), dtype=jnp.float32) * s
        W2 = jax.random.normal(ks[6], (L, D, D), dtype=jnp.float32) * s
        Wa = jax.random.normal(ks[7], (L, 2 * D + 1, 1), dtype=jnp.float32) * s
        return {'attr': attr, 'd': d, 'src': src, 'dst': dst, 'W0': W0, 'W1': W1, 'W2': W2, 'Wa': Wa}
    _L2_gnn_all = _L2_gnn_setup()
    _L2_gnn_in = {k: v for k, v in _L2_gnn_all.items() if k in ('W0', 'W1', 'W2', 'Wa')}
    del _L2_gnn_all

    def _L3_gnn_setup():
        import jax, jax.numpy as jnp
        import numpy as np
        N_NODES = 3125
        N_EDGES = 50000
        IN_DIM = 128
        OUT_DIM = 32
        HEADS = 4
        NEG_SLOPE = 0.2
        EPS = 1e-16

        def _gat_layer(x, edge_index, W, att_src, att_dst, bias, gamma, beta):
            N = x.shape[0]
            H, C = (att_src.shape[1], att_src.shape[2])
            loop = jnp.arange(N, dtype=edge_index.dtype)
            src = jnp.concatenate([edge_index[0], loop])
            dst = jnp.concatenate([edge_index[1], loop])
            h = (x @ W).reshape(N, H, C)
            a_src = jnp.sum(h * att_src, axis=-1)
            a_dst = jnp.sum(h * att_dst, axis=-1)
            logits = a_src[src] + a_dst[dst]
            logits = jnp.where(logits > 0, logits, NEG_SLOPE * logits)
            seg_max = jax.ops.segment_max(logits, dst, num_segments=N)
            e = jnp.exp(logits - seg_max[dst])
            denom = jax.ops.segment_sum(e, dst, num_segments=N)
            alpha = e / (denom[dst] + EPS)
            msgs = h[src] * alpha[:, :, None]
            out = jax.ops.segment_sum(msgs, dst, num_segments=N)
            out = out.reshape(N, H * C) + bias
            mu = jnp.mean(out, axis=-1, keepdims=True)
            var = jnp.var(out, axis=-1, keepdims=True)
            out = (out - mu) * jax.lax.rsqrt(var + 1e-05) * gamma + beta
            return jax.nn.relu(out)
        key = jax.random.key(seed)
        ks = jax.random.split(key, 8)
        x = jax.random.normal(ks[0], (N_NODES, IN_DIM), dtype=jnp.float32)
        edge_index = jax.random.randint(ks[1], (2, N_EDGES), 0, N_NODES, dtype=jnp.int64)
        glorot = 1.0 / np.sqrt(IN_DIM)
        W = jax.random.uniform(ks[2], (IN_DIM, HEADS * OUT_DIM), dtype=jnp.float32, minval=-glorot, maxval=glorot)
        ga = 1.0 / np.sqrt(OUT_DIM)
        att_src = jax.random.uniform(ks[3], (1, HEADS, OUT_DIM), dtype=jnp.float32, minval=-ga, maxval=ga)
        att_dst = jax.random.uniform(ks[4], (1, HEADS, OUT_DIM), dtype=jnp.float32, minval=-ga, maxval=ga)
        bias = jnp.zeros((HEADS * OUT_DIM,), dtype=jnp.float32)
        gamma = jnp.ones((HEADS * OUT_DIM,), dtype=jnp.float32)
        beta = jnp.zeros((HEADS * OUT_DIM,), dtype=jnp.float32)
        return {'x': x, 'edge_index': edge_index, 'W': W, 'att_src': att_src, 'att_dst': att_dst, 'bias': bias, 'gamma': gamma, 'beta': beta}
    _L3_gnn_all = _L3_gnn_setup()
    _L3_gnn_in = {k: v for k, v in _L3_gnn_all.items() if k in ('W', 'att_src', 'att_dst', 'bias', 'gamma', 'beta')}
    del _L3_gnn_all
    return {'x': x, 'src': src, 'dst': dst, 'edge_weight': edge_weight, 'edge_weight1': edge_weight1, 'L0_gnn_W_in_w': _L0_gnn_in['W_in_w'], 'L0_gnn_W_in_b': _L0_gnn_in['W_in_b'], 'L0_gnn_W_upd_w': _L0_gnn_in['W_upd_w'], 'L0_gnn_W_upd_b': _L0_gnn_in['W_upd_b'], 'L0_gnn_W_out_w': _L0_gnn_in['W_out_w'], 'L0_gnn_W_out_b': _L0_gnn_in['W_out_b'], 'L0_gnn_ln1_g': _L0_gnn_in['ln1_g'], 'L0_gnn_ln1_b': _L0_gnn_in['ln1_b'], 'L0_gnn_ln2_g': _L0_gnn_in['ln2_g'], 'L0_gnn_ln2_b': _L0_gnn_in['ln2_b'], 'L0_gnn_ffn1_w': _L0_gnn_in['ffn1_w'], 'L0_gnn_ffn1_b': _L0_gnn_in['ffn1_b'], 'L0_gnn_ffn2_w': _L0_gnn_in['ffn2_w'], 'L0_gnn_ffn2_b': _L0_gnn_in['ffn2_b'], 'L1_gnn_W1': _L1_gnn_in['W1'], 'L1_gnn_W2': _L1_gnn_in['W2'], 'L1_gnn_b1': _L1_gnn_in['b1'], 'L1_gnn_b2': _L1_gnn_in['b2'], 'L2_gnn_W0': _L2_gnn_in['W0'], 'L2_gnn_W1': _L2_gnn_in['W1'], 'L2_gnn_W2': _L2_gnn_in['W2'], 'L2_gnn_Wa': _L2_gnn_in['Wa'], 'L3_gnn_W': _L3_gnn_in['W'], 'L3_gnn_att_src': _L3_gnn_in['att_src'], 'L3_gnn_att_dst': _L3_gnn_in['att_dst'], 'L3_gnn_bias': _L3_gnn_in['bias'], 'L3_gnn_gamma': _L3_gnn_in['gamma'], 'L3_gnn_beta': _L3_gnn_in['beta']}

def reference(x, src, dst, edge_weight, edge_weight1, L0_gnn_W_in_w, L0_gnn_W_in_b, L0_gnn_W_upd_w, L0_gnn_W_upd_b, L0_gnn_W_out_w, L0_gnn_W_out_b, L0_gnn_ln1_g, L0_gnn_ln1_b, L0_gnn_ln2_g, L0_gnn_ln2_b, L0_gnn_ffn1_w, L0_gnn_ffn1_b, L0_gnn_ffn2_w, L0_gnn_ffn2_b, L1_gnn_W1, L1_gnn_W2, L1_gnn_b1, L1_gnn_b2, L2_gnn_W0, L2_gnn_W1, L2_gnn_W2, L2_gnn_Wa, L3_gnn_W, L3_gnn_att_src, L3_gnn_att_dst, L3_gnn_bias, L3_gnn_gamma, L3_gnn_beta):
    import jax
    import jax.numpy as jnp

    def _L0_gnn_ref(x, edge_index, W_in_w, W_in_b, W_upd_w, W_upd_b, W_out_w, W_out_b, ln1_g, ln1_b, ln2_g, ln2_b, ffn1_w, ffn1_b, ffn2_w, ffn2_b):
        import jax, jax.numpy as jnp
        import numpy as np
        N, DIM, K = (50000, 128, 9)
        FFN = 4 * DIM
        EPS = 1e-05

        def layer_norm(x, g, b):
            mu = jnp.mean(x, axis=-1, keepdims=True)
            var = jnp.mean(jnp.square(x - mu), axis=-1, keepdims=True)
            return (x - mu) * jax.lax.rsqrt(var + EPS) * g + b
        src, dst = (edge_index[0], edge_index[1])
        n = x.shape[0]
        h = x @ W_in_w + W_in_b
        diff = h[src] - h[dst]
        seg_max = jax.ops.segment_max(diff, dst, num_segments=n)
        counts = jax.ops.segment_sum(jnp.ones_like(dst, jnp.int32), dst, num_segments=n)
        max_diff = jnp.where((counts > 0)[:, None], seg_max, 0.0)
        h = jnp.concatenate([h, max_diff], axis=-1) @ W_upd_w + W_upd_b
        h = h @ W_out_w + W_out_b
        x = layer_norm(x + h, ln1_g, ln1_b)
        f = jax.nn.gelu(x @ ffn1_w + ffn1_b, approximate=False) @ ffn2_w + ffn2_b
        return layer_norm(x + f, ln2_g, ln2_b)

    def _L1_gnn_ref(ego_embeddings, W1, W2, b1, b2, adj_vals, src, dst):
        import jax, jax.numpy as jnp
        import numpy as np
        N = 3125
        E = 50000
        D = 128
        NEG_SLOPE = 0.2
        EPS = 1e-12
        msgs = ego_embeddings[src] * adj_vals[:, None]
        lap = jax.ops.segment_sum(msgs, dst, num_segments=ego_embeddings.shape[0])
        first = (ego_embeddings + lap) @ W1 + b1
        second = ego_embeddings * lap @ W2 + b2
        out = jax.nn.leaky_relu(first + second, negative_slope=NEG_SLOPE)
        norm = jnp.sqrt(jnp.sum(out * out, axis=1, keepdims=True))
        return out / jnp.maximum(norm, EPS)

    def _L2_gnn_ref(attr, d, src, dst, W0, W1, W2, Wa):
        import jax, jax.numpy as jnp
        import numpy as np

        def _gat_layer(h, d, src, dst, W0_l, W1_l, W2_l, Wa_l, N):
            t = d @ W0_l
            z = h @ W1_l
            z_i = h @ W2_l
            z_src = z[src]
            z_dst = z[dst]
            e = jax.nn.leaky_relu(jnp.concatenate([z_src, z_dst, t], axis=1) @ Wa_l)[:, 0]
            m = jax.ops.segment_max(e, dst, num_segments=N)
            m = jnp.where(jnp.isfinite(m), m, 0.0)
            ex = jnp.exp(e - m[dst])
            denom = jax.ops.segment_sum(ex, dst, num_segments=N)
            alpha = ex / denom[dst]
            z_neighbor = jax.ops.segment_sum(z_src * alpha[:, None], dst, num_segments=N)
            return jax.nn.relu(z_i + z_neighbor)
        N = attr.shape[0]
        L = W0.shape[0]
        h = attr
        for l in range(L):
            h = _gat_layer(h, d, src, dst, W0[l], W1[l], W2[l], Wa[l], N)
        return h

    def _L3_gnn_ref(x, edge_index, W, att_src, att_dst, bias, gamma, beta):
        import jax, jax.numpy as jnp
        import numpy as np
        N_NODES = 3125
        N_EDGES = 50000
        IN_DIM = 128
        OUT_DIM = 32
        HEADS = 4
        NEG_SLOPE = 0.2
        EPS = 1e-16

        def _gat_layer(x, edge_index, W, att_src, att_dst, bias, gamma, beta):
            N = x.shape[0]
            H, C = (att_src.shape[1], att_src.shape[2])
            loop = jnp.arange(N, dtype=edge_index.dtype)
            src = jnp.concatenate([edge_index[0], loop])
            dst = jnp.concatenate([edge_index[1], loop])
            h = (x @ W).reshape(N, H, C)
            a_src = jnp.sum(h * att_src, axis=-1)
            a_dst = jnp.sum(h * att_dst, axis=-1)
            logits = a_src[src] + a_dst[dst]
            logits = jnp.where(logits > 0, logits, NEG_SLOPE * logits)
            seg_max = jax.ops.segment_max(logits, dst, num_segments=N)
            e = jnp.exp(logits - seg_max[dst])
            denom = jax.ops.segment_sum(e, dst, num_segments=N)
            alpha = e / (denom[dst] + EPS)
            msgs = h[src] * alpha[:, :, None]
            out = jax.ops.segment_sum(msgs, dst, num_segments=N)
            out = out.reshape(N, H * C) + bias
            mu = jnp.mean(out, axis=-1, keepdims=True)
            var = jnp.var(out, axis=-1, keepdims=True)
            out = (out - mu) * jax.lax.rsqrt(var + 1e-05) * gamma + beta
            return jax.nn.relu(out)
        return _gat_layer(x, edge_index, W, att_src, att_dst, bias, gamma, beta)
    edge_index = jnp.stack([src, dst])
    x = _layernorm(x + _L0_gnn_ref(x, edge_index, L0_gnn_W_in_w, L0_gnn_W_in_b, L0_gnn_W_upd_w, L0_gnn_W_upd_b, L0_gnn_W_out_w, L0_gnn_W_out_b, L0_gnn_ln1_g, L0_gnn_ln1_b, L0_gnn_ln2_g, L0_gnn_ln2_b, L0_gnn_ffn1_w, L0_gnn_ffn1_b, L0_gnn_ffn2_w, L0_gnn_ffn2_b), axis=-1)
    x = _layernorm(x + _L1_gnn_ref(x, L1_gnn_W1, L1_gnn_W2, L1_gnn_b1, L1_gnn_b2, edge_weight, src, dst), axis=-1)
    x = _layernorm(x + _L2_gnn_ref(x, edge_weight1, src, dst, L2_gnn_W0, L2_gnn_W1, L2_gnn_W2, L2_gnn_Wa), axis=-1)
    x = _layernorm(x + _L3_gnn_ref(x, edge_index, L3_gnn_W, L3_gnn_att_src, L3_gnn_att_dst, L3_gnn_bias, L3_gnn_gamma, L3_gnn_beta), axis=-1)
    return x

_drawn_inputs = setup_inputs


def setup_inputs(seed=0):
    import zlib

    import numpy as np

    out = dict(_drawn_inputs(seed))
    spreads = {'L0_gnn_W_in_b': (0.0, 0.27),
     'L0_gnn_W_upd_b': (0.0, 0.1),
     'L0_gnn_W_out_b': (0.0, 0.1),
     'L0_gnn_ln1_g': (1.0, 0.2),
     'L0_gnn_ln1_b': (0.0, 0.1),
     'L0_gnn_ln2_g': (1.0, 0.2),
     'L0_gnn_ln2_b': (0.0, 0.1),
     'L0_gnn_ffn1_b': (0.0, 0.1),
     'L0_gnn_ffn2_b': (0.0, 0.1),
     'L1_gnn_b1': (0.0, 2.0),
     'L1_gnn_b2': (0.0, 2.0),
     'L3_gnn_bias': (0.0, 0.1),
     'L3_gnn_gamma': (1.0, 0.2),
     'L3_gnn_beta': (0.0, 0.1)}
    factors = {'edge_weight': 30.151, 'edge_weight1': 8.0, 'L2_gnn_W0': 8.0, 'L3_gnn_att_dst': 3.795}
    for name, (base, spread) in spreads.items():
        noise = np.random.default_rng([zlib.crc32(name.encode()), seed]).standard_normal(out[name].shape)
        drawn = base * np.exp(spread * noise) if base else spread * noise
        out[name] = jnp.asarray(drawn.astype(out[name].dtype))
    for name, factor in factors.items():
        out[name] = (out[name] * factor).astype(out[name].dtype)
    return out
```

```python
from contextlib import ExitStack, contextmanager

import numpy as np

import concourse.bass as bass
from concourse import mybir
from concourse.alu_op_type import AluOpType as ALU

F32 = mybir.dt.float32
BF16 = mybir.dt.bfloat16
I32 = mybir.dt.int32
ACT = mybir.ActivationFunctionType
AX_X = mybir.AxisListType.X

P = 128
N = 3125
E = 100000
D = 128
HEADS, HD = 4, 32
NT = -(-N // P)
NP = NT * P
TAIL = N - (NT - 1) * P
U = 16
TILES = -(-E // (P * U)) * U
ITERS = TILES // U
EP = TILES * P
J = EP // P
CH = 7
CT = TILES // CH
LASTB = NP - 2 * P
BANK = 512
NBANK = -(-NP // BANK)
BIG = 1e30
LOWEST = -3.0e38
PADDST = 4095
FARIDX = 8192
G = 4
NG = U // G
PARTS = 3
STEPS = (P, PARTS, PARTS * HEADS, PARTS * 2 * HEADS)
EXTRA = NP
TURN = 7 * BANK
H8 = U // 2


class Signal:

    def __init__(self, sem):
        self.sem, self.at = sem, 0

    def up(self, n=1):
        self.at += n
        return self.at


def rows_view(t):
    return t[:].rearrange("p (i f) -> p i f", f=D)


def column(t):
    return t.rearrange("(n o) -> n o", o=1)


def on_all(t):
    return t.rearrange("(o n) -> o n", o=1).to_broadcast([P, t.shape[0]])


def bank(b):
    return b * BANK, min(NP, (b + 1) * BANK)


class Kernel:
    def __init__(self, nc, ctx, args, out):
        self.nc, self.ctx, self.a, self.out = nc, ctx, args, out
        self.names = 0
        signal = lambda name: Signal(ctx.enter_context(nc.semaphore(name)))
        self.pe_done, self.dve_done = signal("pe_done"), signal("dve_done")
        self.act_done, self.pool_done = signal("act_done"), signal("pool_done")
        self.dve_chain = signal("dve_chain")
        self.loaded, self.stored = signal("loaded"), signal("stored")
        self.idx_staged, self.group_begun = signal("idx_staged"), signal("group_begun")
        self.ind_built, self.tiles_summed = signal("ind_built"), signal("tiles_summed")
        self.rows_moved = signal("rows_moved")
        self.rows_turned, self.scanned = signal("rows_turned"), signal("scanned")
        self.scan_turned, self.turned_out = signal("scan_turned"), signal("turned_out")
        self.hot_built, self.picked, self.pick_read = signal("hot_built"), signal("picked"), signal("pick_read")
        self.gathered = [Signal(ctx.enter_context(nc.semaphore(f"gathered{g}"))) for g in range(NG)]
        self.mask_in = [Signal(ctx.enter_context(nc.semaphore(f"mask_in{g}"))) for g in range(NG)]
        self.lo_in = [Signal(ctx.enter_context(nc.semaphore(f"lo_in{g}"))) for g in range(2)]
        self.rel_in = [Signal(ctx.enter_context(nc.semaphore(f"rel_in{g}"))) for g in range(2)]
        self.ps = ctx.enter_context(nc.psum_tensor("ps", [P, 8 * BANK], F32))

    def sb(self, name, shape, dt=F32):
        self.names += 1
        return self.ctx.enter_context(self.nc.sbuf_tensor(f"{name}_{self.names}", shape, dt))

    @contextmanager
    def scope(self):
        outer = self.ctx
        with ExitStack() as self.ctx:
            yield
        self.ctx = outer

    def dram(self, name, shape, dt=F32):
        return self.nc.dram_tensor(name, shape, dt, kind="Internal").ap()

    def link(self, eng, ins):
        eng_wait = self.dve_chain.up()
        ins.then_inc(self.dve_chain.sem, 1)
        eng.wait_ge(self.dve_chain.sem, eng_wait)

    def load(self, pairs):
        with self.nc.Block() as block:
            @block.sync
            def _(sp):
                for to, of in pairs:
                    sp.dma_start(to, of).then_inc(self.loaded.sem, 16)
                    self.loaded.up(16)
                sp.wait_ge(self.loaded.sem, self.loaded.at)

    def _drain_banks(self, block, ready, vec, act):
        @block.vector
        def _(dve):
            for b in range(NBANK):
                if b % 2 == 0 or act is None:
                    dve.wait_ge(self.pe_done.sem, ready[b])
                    vec(*bank(b)).then_inc(self.dve_done.sem, 1)
                    self.dve_done.up()
            dve.wait_ge(self.dve_done.sem, self.dve_done.at)

        @block.scalar
        def _(sc):
            if act is None:
                return
            for b in range(NBANK):
                if b % 2 == 1 or vec is None:
                    sc.wait_ge(self.pe_done.sem, ready[b])
                    act(*bank(b)).then_inc(self.act_done.sem, 1)
                    self.act_done.up()
            sc.wait_ge(self.act_done.sem, self.act_done.at)

    def turn(self, to, of, add=None):
        nc, ps = self.nc, self.ps
        ready = []
        with nc.Block() as block:
            @block.tensor
            def _(pe):
                for i in range(NT):
                    c = slice(i * P, (i + 1) * P)
                    nc.tensor.transpose(ps[:, c], of[:, c], self.ident[:]).then_inc(self.pe_done.sem, 1)
                    self.pe_done.up()
                    if i % 4 == 3 or i == NT - 1:
                        ready.append(self.pe_done.at)

            if add is None:
                self._drain_banks(block, ready,
                                  lambda a, b: nc.vector.tensor_copy(to[:, a:b], ps[:, a:b]),
                                  lambda a, b: nc.scalar.copy(to[:, a:b], ps[:, a:b]))
            else:
                self._drain_banks(block, ready,
                                  lambda a, b: nc.vector.tensor_tensor(to[:, a:b], ps[:, a:b], add[:, a:b], ALU.add),
                                  None)

    def linear_t(self, to, terms, bias=None, gelu=False):
        nc, ps = self.nc, self.ps
        ready = []
        with nc.Block() as block:
            @block.tensor
            def _(pe):
                for b in range(NBANK):
                    lo, hi = bank(b)
                    for n, (w, x) in enumerate(terms):
                        last = nc.tensor.matmul(ps[:, lo:hi], w, x[:, lo:hi], start=n == 0, stop=n == len(terms) - 1)
                    last.then_inc(self.pe_done.sem, 1)
                    ready.append(self.pe_done.up())

            if gelu:
                @block.scalar
                def _(sc):
                    for b in range(NBANK):
                        lo, hi = bank(b)
                        sc.wait_ge(self.pe_done.sem, ready[b])
                        nc.scalar.activation(to[:, lo:hi], ps[:, lo:hi], ACT.Gelu, bias=bias).then_inc(self.act_done.sem, 1)
                        self.act_done.up()
                    sc.wait_ge(self.act_done.sem, self.act_done.at)
            elif bias is None:
                self._drain_banks(block, ready,
                                  lambda a, b: nc.vector.tensor_copy(to[:, a:b], ps[:, a:b]),
                                  lambda a, b: nc.scalar.copy(to[:, a:b], ps[:, a:b]))
            else:
                self._drain_banks(block, ready,
                                  lambda a, b: nc.vector.tensor_scalar(to[:, a:b], ps[:, a:b], bias, None, ALU.add),
                                  lambda a, b: nc.scalar.activation(to[:, a:b], ps[:, a:b], ACT.Identity, bias=bias))

    def linear_rows(self, to, x_t, w, width):
        nc = self.nc
        per = BANK // width if width < P else 4
        per = min(per, 4)
        ps = self.ps[:].rearrange("p (b k c) -> p b k c", b=8, k=4)
        ready = []
        with nc.Block() as block:
            @block.tensor
            def _(pe):
                for i in range(NT):
                    nc.tensor.matmul(ps[:, i // 4, i % 4, 0:width], x_t[:, i * P:(i + 1) * P], w,
                                     start=True, stop=True).then_inc(self.pe_done.sem, 1)
                    self.pe_done.up()
                    if i % 4 == 3 or i == NT - 1:
                        ready.append(self.pe_done.at)

            @block.vector
            def _(dve):
                for b in range(NBANK):
                    k = min(4, NT - 4 * b)
                    dve.wait_ge(self.pe_done.sem, ready[b])
                    nc.vector.tensor_copy(to[:, 4 * b:4 * b + k, :], ps[:, b, 0:k, 0:width]).then_inc(self.dve_done.sem, 1)
                    self.dve_done.up()
                dve.wait_ge(self.dve_done.sem, self.dve_done.at)

    def layer_norm(self, to, x, eps, gamma=None, beta=None):
        with self.scope():
            self._layer_norm(to, x, eps, gamma, beta, self.sb("squares", [P, NP]))

    def _layer_norm(self, to, x, eps, gamma, beta, squares):
        nc = self.nc
        st = self.stat
        view = lambda t: t[:].rearrange("p (i f) -> p i f", f=D)
        bc = lambda c: st[:, c, :].unsqueeze(2).to_broadcast([P, NT, D])
        row = lambda r: r[:].unsqueeze(1).to_broadcast([P, NT, D])
        centred, squared, rooted = self.dve_done.at + 1, self.act_done.at + 1, self.act_done.at + 2
        with nc.Block() as block:
            @block.vector
            def _(dve):
                self.link(dve, nc.vector.tensor_reduce(st[:, 0, :], view(x), AX_X, ALU.add))
                self.link(dve, nc.vector.tensor_scalar(st[:, 1, :], st[:, 0, :], 1.0 / D, None, ALU.mult))
                nc.vector.tensor_tensor(view(to), view(x), bc(1), ALU.subtract).then_inc(self.dve_done.sem, 1)
                self.dve_done.up()
                dve.wait_ge(self.act_done.sem, squared)
                self.link(dve, nc.vector.tensor_reduce(st[:, 2, :], view(squares), AX_X, ALU.add))
                nc.vector.tensor_scalar(st[:, 3, :], st[:, 2, :], 1.0 / D, eps, ALU.mult, ALU.add).then_inc(self.dve_done.sem, 1)
                self.dve_done.up()
                dve.wait_ge(self.act_done.sem, rooted)
                self.link(dve, nc.vector.reciprocal(st[:, 5, :], st[:, 4, :]))
                self.link(dve, nc.vector.tensor_tensor(view(to), view(to), bc(5), ALU.mult))
                if gamma is not None:
                    self.link(dve, nc.vector.tensor_tensor(view(to), view(to), row(gamma), ALU.mult))
                    self.link(dve, nc.vector.tensor_tensor(view(to), view(to), row(beta), ALU.add))

            @block.scalar
            def _(sc):
                sc.wait_ge(self.dve_done.sem, centred)
                nc.scalar.activation(squares[:], to[:], ACT.Square).then_inc(self.act_done.sem, 1)
                sc.wait_ge(self.dve_done.sem, centred + 1)
                nc.scalar.activation(st[:, 4, :], st[:, 3, :], ACT.Sqrt).then_inc(self.act_done.sem, 1)
                self.act_done.up(2)

    def dve_steps(self, program):
        with self.nc.Block() as block:
            @block.vector
            def _(dve):
                program(lambda ins: self.link(dve, ins))

    def constants(self):
        nc = self.nc
        self.ident = self.sb("ident", [P, P])
        self.before = self.sb("before", [P, P])
        self.iota_w = self.sb("iota_w", [P, 2 * P])
        self.iota_p = self.sb("iota_p", [P, 2])
        self.iota_h = self.sb("iota_h", [P, NT], BF16)
        self.zeros = self.sb("zeros", [P, BANK])
        with self.scope():
            self._fill_constants(self.sb("iw", [P, 2 * P], I32), self.sb("ip", [P, 2], I32))

    def _fill_constants(self, iw, ip):
        nc = self.nc
        made = self.pool_done.at
        with nc.Block() as block:
            @block.gpsimd
            def _(pool):
                nc.gpsimd.memset(self.ident[:], 0.0).then_inc(self.pool_done.sem, 1)
                nc.gpsimd.memset(self.before[:], 0.0).then_inc(self.pool_done.sem, 1)
                pool.wait_ge(self.pool_done.sem, made + 2)
                nc.gpsimd.affine_select(out=self.ident[:], in_=self.ident[:], compare_op=ALU.not_equal, fill=1.0, base=0,
                                        pattern=[[-1, P]], channel_multiplier=1).then_inc(self.pool_done.sem, 1)
                nc.gpsimd.affine_select(out=self.before[:], in_=self.before[:], compare_op=ALU.is_ge, fill=1.0, base=0,
                                        pattern=[[-1, P]], channel_multiplier=1).then_inc(self.pool_done.sem, 1)
                nc.gpsimd.iota(iw[:], pattern=[[1, 2 * P]], base=0, channel_multiplier=0).then_inc(self.pool_done.sem, 1)
                nc.gpsimd.iota(ip[:], pattern=[[P, 2]], base=0, channel_multiplier=1).then_inc(self.pool_done.sem, 1)
                self.pool_done.up(6)
                pool.wait_ge(self.pool_done.sem, self.pool_done.at)

            @block.vector
            def _(dve):
                self.link(dve, nc.vector.memset(self.zeros[:], 0.0))
                dve.wait_ge(self.pool_done.sem, self.pool_done.at)
                self.link(dve, nc.vector.tensor_copy(self.iota_w[:], iw[:]))
                self.link(dve, nc.vector.tensor_copy(self.iota_p[:], ip[:]))
                self.link(dve, nc.vector.tensor_copy(self.iota_h[:], iw[:, 0:NT]))

    def c_to_a(self, pairs):
        nc = self.nc
        ps = self.ps[:].rearrange("p (h c e) -> p h c e", h=4, c=8)
        turned = []
        drained = self.dve_done.at
        with nc.Block() as block:
            @block.tensor
            def _(pe):
                for n, (to, of) in enumerate(pairs):
                    if n >= 4:
                        pe.wait_ge(self.dve_done.sem, drained + n - 3)
                    for c in range(CH):
                        last = nc.tensor.transpose(ps[:, n % 4, c, 0:CT], of[:, c, :], self.ident[0:CT, 0:CT])
                    last.then_inc(self.pe_done.sem, 1)
                    turned.append(self.pe_done.up())

            @block.vector
            def _(dve):
                for n, (to, of) in enumerate(pairs):
                    dve.wait_ge(self.pe_done.sem, turned[n])
                    nc.vector.tensor_copy(to.rearrange("p (c t) -> p c t", c=CH), ps[:, n % 4, 0:CH, 0:CT]).then_inc(self.dve_done.sem, 1)
                    self.dve_done.up()
                dve.wait_ge(self.dve_done.sem, self.dve_done.at)

    def a_to_c(self, pairs):
        nc = self.nc
        ps = self.ps[:].rearrange("p (h c e) -> p h c e", h=4, c=8)
        turned = []
        drained = self.dve_done.at
        with nc.Block() as block:
            @block.tensor
            def _(pe):
                for n, (to, of) in enumerate(pairs):
                    if n >= 4:
                        pe.wait_ge(self.dve_done.sem, drained + n - 3)
                    for c in range(CH):
                        last = nc.tensor.transpose(ps[0:CT, n % 4, c, :], of[:, c * CT:(c + 1) * CT], self.ident[:])
                    last.then_inc(self.pe_done.sem, 1)
                    turned.append(self.pe_done.up())

            @block.vector
            def _(dve):
                for n, (to, of) in enumerate(pairs):
                    dve.wait_ge(self.pe_done.sem, turned[n])
                    nc.vector.tensor_copy(to, ps[0:CT, n % 4, 0:CH, :]).then_inc(self.dve_done.sem, 1)
                    self.dve_done.up()
                dve.wait_ge(self.dve_done.sem, self.dve_done.at)

    def edge_lists(self):
        nc, a = self.nc, self.a
        self.dstx = self.dram("dstx", [EP + 2], I32)
        self.srcx = self.dram("srcx", [EP], I32)
        self.wx = self.dram("wx", [EP])
        self.w1x = self.dram("w1x", [EP])
        self.agg_max = self.dram("agg_max", [NP, D])
        self.agg = self.dram("agg", [NP, D])
        self.agg3 = self.dram("agg3", [NP, D + HEADS])
        pad = EP - E
        ends = self.sb("ends", [1, pad + 2], I32)
        zi = self.sb("zi", [1, pad], I32)
        low = self.sb("low", [P, D])
        none3 = self.sb("none3", [P, D + HEADS])

        @self.dve_steps
        def _(link):
            link(nc.vector.memset(ends[0:1, 0:1], -1))
            link(nc.vector.memset(ends[0:1, 1:], PADDST))
            link(nc.vector.memset(ends[0:1, pad + 1:], PADDST + 1))
            link(nc.vector.memset(zi[:], 0))
            link(nc.vector.memset(low[:], LOWEST))
            link(nc.vector.memset(none3[:, 0:D], 0.0))
            link(nc.vector.memset(none3[:, D:], 1.0))
        row = lambda v: v.rearrange("(a n) -> a n", a=1)
        wide = lambda v: v.rearrange("(a n) -> a n", a=16)
        pairs = [(wide(self.dstx[1:E + 1]), wide(a["dst"])), (wide(self.srcx[0:E]), wide(a["src"])),
                 (wide(self.wx[0:E]), wide(a["edge_weight"])),
                 (wide(self.w1x[0:E]), wide(a["edge_weight1"].rearrange("n o -> (n o)"))),
                 (row(self.dstx[0:1]), ends[0:1, 0:1]), (row(self.dstx[E + 1:]), ends[0:1, 1:]),
                 (row(self.srcx[E:]), zi[:]),
                 (row(self.wx[E:]), self.zeros[0:1, 0:pad]), (row(self.w1x[E:]), self.zeros[0:1, 0:pad])]
        tiles = lambda v: v.rearrange("(i p) f -> p i f", p=P)
        pairs += [(tiles(self.agg_max), low[:].unsqueeze(1).to_broadcast([P, NT, D])),
                  (tiles(self.agg), self.zeros[:, 0:D].unsqueeze(1).to_broadcast([P, NT, D])),
                  (tiles(self.agg3), none3[:].unsqueeze(1).to_broadcast([P, NT, D + HEADS]))]
        self.load(pairs)

    def edge_structure(self):
        nc = self.nc
        by_b = lambda v: v.rearrange("(p j) -> p j", p=P)
        by_c = lambda v: v.rearrange("(c t e) -> t c e", c=CH, t=CT)
        self.rel_a, self.end_a, self.w_a = (self.sb(n, [P, TILES]) for n in ("rel_a", "end_a", "w_a"))
        self.dst3 = self.sb("dst3", [P, PARTS, TILES], BF16)
        self.idx_a = self.sb("idx_a", [P, TILES], I32)
        self.hi16_a = self.sb("hi16_a", [P, TILES], BF16)
        self.base = self.sb("base", [1, 2, TILES], I32)
        self.w1_b = self.sb("w1_b", [P, J])
        self.b = {n: self.sb("b_" + n, [P, J]) for n in
                  ("go_f", "go_g", "neg_f", "neg_g", "open_f", "open_g", "cut_f", "cut_g")}
        self.cut_row = self.sb("cut_row", [HEADS, 4, P])
        with self.scope():
            self._edge_structure(by_b, by_c)

    def _edge_structure(self, by_b, by_c):
        nc = self.nc
        cur, prev, nxt = (self.sb(n, [P, J], I32) for n in ("cur", "prev", "nxt"))
        self.load([(cur[:], by_b(self.dstx[1:EP + 1])), (prev[:], by_b(self.dstx[0:EP])), (nxt[:], by_b(self.dstx[2:EP + 2])),
                   (self.w1_b[:], by_b(self.w1x))])
        b = dict(self.b, start=self.sb("start", [P, J]), end=self.sb("end", [P, J]))
        ones, zeros = self.sb("ones_j", [P, J]), self.sb("zeros_j", [P, J])
        self.cut_col = self.sb("cut_col", [P, 2, HEADS])
        rank = self.sb("rank", [P, J])
        off = self.sb("off", [P, 1])
        neg16 = self.sb("neg16", [P, J], BF16)
        rev = lambda t: t[:, ::-1]

        @self.dve_steps
        def _(link):
            link(nc.vector.memset(ones[:], 1.0))
            link(nc.vector.memset(zeros[:], 0.0))
            link(nc.vector.tensor_tensor(b["start"][:], cur[:], prev[:], ALU.not_equal))
            link(nc.vector.tensor_tensor(b["end"][:], cur[:], nxt[:], ALU.not_equal))
            link(nc.vector.tensor_scalar(b["go_f"][:], b["start"][:], -1.0, 1.0, ALU.mult, ALU.add))
            link(nc.vector.tensor_scalar(b["go_g"][:], b["end"][:], -1.0, 1.0, ALU.mult, ALU.add))
            link(nc.vector.tensor_scalar(b["neg_f"][:], b["start"][:], -BIG, None, ALU.mult))
            link(nc.vector.tensor_scalar(b["neg_g"][:], b["end"][:], -BIG, None, ALU.mult))
            link(nc.vector.tensor_copy(neg16[:], b["neg_f"][:]))
            link(nc.vector.tensor_tensor_scan(out=b["open_f"][:], data0=b["go_f"][:], data1=zeros[:], initial=1.0,
                                              op0=ALU.mult, op1=ALU.add))
            link(nc.vector.tensor_tensor_scan(out=rev(b["open_g"]), data0=rev(b["go_g"]), data1=zeros[:], initial=1.0,
                                              op0=ALU.mult, op1=ALU.add))
            link(nc.vector.tensor_scalar(b["cut_f"][:], b["open_f"][:], BIG, -BIG, ALU.mult, ALU.add))
            link(nc.vector.tensor_scalar(b["cut_g"][:], b["open_g"][:], BIG, -BIG, ALU.mult, ALU.add))
            link(nc.vector.tensor_tensor_scan(out=rank[:], data0=ones[:], data1=b["start"][:], initial=0.0,
                                              op0=ALU.mult, op1=ALU.add))
            link(nc.vector.tensor_copy(self.cut_col[:, 0, :], b["open_f"][:, J - 1:J].to_broadcast([P, HEADS])))
            link(nc.vector.tensor_copy(self.cut_col[:, 1, :], b["open_g"][:, 0:1].to_broadcast([P, HEADS])))
        ps = self.ps
        summed, = [self.pe_done.at + 1]
        with nc.Block() as block:
            @block.tensor
            def _(pe):
                nc.tensor.matmul(ps[:, 0:1], self.before[:], rank[:, J - 1:J], start=True, stop=True)
                nc.tensor.matmul(ps[0:HEADS, BANK:BANK + P], self.cut_col[:, 0, :], self.ident[:], start=True, stop=True)
                nc.tensor.matmul(ps[0:HEADS, 2 * BANK:2 * BANK + P], self.cut_col[:, 1, :], self.ident[:],
                                 start=True, stop=True).then_inc(self.pe_done.sem, 1)
                self.pe_done.up()

            @block.vector
            def _(dve):
                dve.wait_ge(self.pe_done.sem, summed)
                self.link(dve, nc.vector.tensor_copy(off[:], ps[:, 0:1]))
                self.link(dve, nc.vector.tensor_scalar(rank[:], rank[:], off[:, 0:1], -1.0, ALU.add, ALU.add))
                for n in range(2):
                    row = ps[0:HEADS, (n + 1) * BANK:(n + 1) * BANK + P]
                    self.link(dve, nc.vector.tensor_copy(self.cut_row[:, n, :], row))
                    self.link(dve, nc.vector.tensor_scalar(self.cut_row[:, 2 + n, :], row, BIG, -BIG, ALU.mult, ALU.add))
        rank_d, end_d = self.dram("rank_d", [EP]), self.dram("end_d", [EP])
        self.neg_d = self.dram("neg_d", [EP], BF16)
        self.load([(by_b(rank_d), rank[:]), (by_b(end_d), b["end"][:]), (by_b(self.neg_d), neg16[:])])
        rank_c, end_c, w_c = (self.sb(n, [CT, CH, P]) for n in ("rank_c", "end_c", "w_c"))
        src_c, dst_c = (self.sb(n, [CT, CH, P], I32) for n in ("src_c", "dst_c"))
        self.load([(rank_c[:], by_c(rank_d)), (end_c[:], by_c(end_d)), (w_c[:], by_c(self.wx)),
                   (src_c[:], by_c(self.srcx)), (dst_c[:], by_c(self.dstx[1:EP + 1]))])
        base_i = self.sb("base_i", [CT, CH], I32)
        bases = self.sb("bases", [CT, len(STEPS), CH], I32)
        base_f = self.sb("base_f", [CT, CH])
        lo_i, hi_i = (self.sb(n, [CT, CH, P], I32) for n in ("lo_i", "hi_i"))
        src_f, hi_f, dst_f, rel_f = (self.sb(n, [CT, CH, P]) for n in ("src_f", "hi_f", "dst_f", "rel_f"))
        lo16, rel16 = (self.sb(n, [CT, CH, P], BF16) for n in ("lo16", "rel16"))
        v = nc.vector

        @self.dve_steps
        def _(link):
            link(v.tensor_copy(base_i[:], rank_c[:, :, 0]))
            link(v.tensor_scalar(base_i[:], base_i[:], 7, 7, ALU.logical_shift_right, ALU.logical_shift_left))
            link(v.tensor_scalar(base_f[:], base_i[:], float(LASTB), None, ALU.min))
            for n, k in enumerate(STEPS):
                link(v.tensor_scalar(bases[:, n, :], base_f[:], k / P, None, ALU.mult))
            link(v.tensor_tensor(rel_f[:], rank_c[:], base_f[:].unsqueeze(2).to_broadcast([CT, CH, P]), ALU.subtract))
            link(v.tensor_copy(rel16[:], rel_f[:]))
            link(v.tensor_scalar(lo_i[:], src_c[:], P - 1, None, ALU.bitwise_and))
            link(v.tensor_scalar(hi_i[:], src_c[:], 7, None, ALU.logical_shift_right))
            link(v.tensor_copy(lo16[:], lo_i[:]))
            link(v.tensor_copy(hi_f[:], hi_i[:]))
            link(v.tensor_copy(src_f[:], src_c[:]))
            link(v.tensor_scalar(dst_f[:], dst_c[:], 1.0, None, ALU.add))
        base_d = self.dram("base_d", [len(STEPS), TILES], I32)
        self.lo_d, self.rel_d = self.dram("lo_d", [EP], BF16), self.dram("rel_d", [EP], BF16)
        with nc.allow_non_contiguous_dma(reason="784 window bases, once"):
            self.load([(base_d[n].rearrange("(c t o) -> t c o", c=CH, o=1), bases[:, n, :].unsqueeze(2)) for n in range(len(STEPS))]
                      + [(by_c(self.lo_d), lo16[:]), (by_c(self.rel_d), rel16[:])])
        self.base_d = base_d
        self.src_a, self.hi_a, self.dst_a, rest = (self.sb(n, [P, TILES]) for n in ("src_a", "hi_a", "dst_a", "rest"))
        self.c_to_a([(self.rel_a[:], rel_f), (self.end_a[:], end_c), (self.w_a[:], w_c), (self.dst_a[:], dst_f),
                     (self.src_a[:], src_f), (self.hi_a[:], hi_f)])

        @self.dve_steps
        def _(link):
            link(v.tensor_copy(self.idx_a[:], self.src_a[:]))
            link(v.tensor_copy(self.hi16_a[:], self.hi_a[:]))
            self.split(link, self.dst_a[:], [self.dst3[:, n] for n in range(PARTS)], rest[:])

    def _gathers(self, block, table, freed, loops=((0, ITERS, NG, 0),), tile0=0):
        nc = self.nc
        staged0, freed0 = self.idx_staged.at, freed.at

        @block.gpsimd
        def _(pool):
            for lo, hi, slots, skip in loops:
                with pool.Fori(lo, hi) as i:
                    for g in range(NG):
                        pool.wait_ge(freed.sem, freed0 + skip + i * slots + g + 1)
                        nc.gpsimd.tensor_copy(self.idx_now[:, g * G:(g + 1) * G],
                                              self.idx_a[:, bass.ds(tile0 + i * U + g * G, G)]).then_inc(self.idx_staged.sem, 1)
                        pool.wait_ge(self.loaded.sem, self.loaded.at)
                        pool.wait_ge(self.idx_staged.sem, staged0 + 1 + i * NG + g)
                        pool.sem_inc(self.group_begun.sem, 1)
                        for k in range(G):
                            t = g * G + k
                            nc.gpsimd.indirect_dma_start(
                                out=self.rows[:, t, :], out_offset=None, in_=table,
                                in_offset=bass.IndirectOffsetOnAxis(ap=self.idx_now[:, t:t + 1], axis=0),
                            ).then_inc(self.gathered[g].sem, 16)
        self.idx_staged.up(NG * loops[-1][1])

    def _prefetch(self, block, table, tiles):
        nc, iters = self.nc, tiles // U
        gathered0, moved0 = self.gathered[0].at, self.rows_moved.at
        self._gathers(block, table, self.rows_moved, ((0, iters, NG, 0),))

        @block.scalar
        def _(sc):
            sc.sem_inc(self.rows_moved.sem, NG)
            with sc.Fori(0, iters) as i:
                for g in range(NG):
                    sc.wait_ge(self.gathered[g].sem, gathered0 + (i + 1) * 16 * G)
                    nc.scalar.copy(self.early[:, bass.ds(i * U + g * G, G), :],
                                   self.rows[:, g * G:(g + 1) * G, :]).then_inc(self.rows_moved.sem, 1)
        self.rows_moved.up(NG + NG * iters)
        for g in range(NG):
            self.gathered[g].up(16 * G * iters)

    def load_bases(self, width):
        self.load([(self.base[0:1, n, :], self.base_d[k:k + 1, :]) for n, k in ((0, 0), (1, STEPS.index(width)))])

    def split(self, link, of, parts, rest):
        v = self.nc.vector
        link(v.tensor_copy(parts[0], of))
        link(v.tensor_tensor(rest, of, parts[0], ALU.subtract))
        link(v.tensor_copy(parts[1], rest))
        link(v.tensor_tensor(rest, rest, parts[1], ALU.subtract))
        link(v.tensor_copy(parts[2], rest))

    def clear_accumulator(self):
        nc = self.nc
        with nc.Block() as block:
            @block.tensor
            def _(pe):
                for b in range(8):
                    nc.tensor.matmul(self.ps[:, b * BANK:(b + 1) * BANK], self.zeros[:, 0:P], self.zeros[:], start=True, stop=True)

    def _accumulate(self, pe, tile0, buffer, regs, rows, extra, tiles=range(G)):
        nc, ps = self.nc, self.ps
        for k in tiles:
            w = pe.snap(regs[k], min_val=0, max_val=LASTB)
            for half in range(2):
                ind = self.ind[:, buffer, k, half * P:(half + 1) * P]
                last = nc.tensor.matmul(ps[:, bass.ds(w + half * P, D)], ind, rows[k], start=False, stop=True, skip_group_check=True)
            if extra is not None:
                values, width = extra
                x = pe.snap(regs[G + k], min_val=0, max_val=LASTB // P * width)
                for half in range(2):
                    ind = self.ind[:, buffer, k, half * P:(half + 1) * P].bitcast(BF16)[:, 1::2]
                    last = nc.tensor.matmul(ps[:, bass.ds(x + (EXTRA + half * width), width)], ind,
                                            values[:, :, bass.ds(tile0 + k, 1)], start=False, stop=True, skip_group_check=True)
        if tiles[-1] == G - 1:
            last.then_inc(self.tiles_summed.sem, 1)

    def _bases(self, pe, tile0, regs, extra):
        pe.load(regs[:G], self.base[0:1, 0, bass.ds(tile0, G)])
        if extra is not None:
            pe.load(regs[G:], self.base[0:1, 1, bass.ds(tile0, G)])

    def sum_pass(self, table, alpha, heads=False, extra=None, early=0):
        with self.scope():
            self.ind = self.sb("ind", [P, 3, G, 2 * P])
            self._sum_pass(table, alpha, heads, extra, early)

    def _ring(self):
        self.idx_now = self.sb("idx_now", [P, U], I32)
        self.rows = self.sb("rows", [P, U, D])

    def _sum_pass(self, table, alpha, heads, extra, early):
        nc = self.nc
        self.clear_accumulator()
        self.load_bases(extra[1] if extra else P)
        iters = ITERS - early // U
        both = min(early // G, iters)
        late = early // G - both
        EARLY = 2
        summed0, built0, gathered0 = self.tiles_summed.at, self.ind_built.at, self.gathered[0].at
        self.tiles_summed.up(NG)
        freed = Signal(self.tiles_summed.sem)
        freed.at = summed0
        loops = ((0, both, NG + 1, 0), (both, iters, NG, both))
        loops = [loop for loop in loops if loop[0] < loop[1]]
        with nc.Block() as block:
            self._gathers(block, table, freed, loops, early)

            @block.vector
            def _(dve):
                dve.sem_inc(self.tiles_summed.sem, NG)

                def build(n, tile0, buffer, rows, ring=None):
                    dve.wait_ge(self.tiles_summed.sem, summed0 + NG - 1 + n)
                    for k in range(G):
                        col = bass.ds(tile0 + k, 1)
                        ind = self.ind[:, buffer, k, :]
                        if heads:
                            last = nc.vector.tensor_scalar(ind, self.iota_w[:], self.rel_a[:, col], None, ALU.is_equal)
                        else:
                            last = nc.vector.tensor_scalar(ind, self.iota_w[:], self.rel_a[:, col], alpha[:, 0, col],
                                                           ALU.is_equal, ALU.mult)
                    if heads:
                        if ring:
                            g, i = ring
                            dve.wait_ge(self.gathered[g].sem, gathered0 + (i + 1) * 16 * G)
                        v = rows.rearrange("p t (h c) -> p t h c", h=HEADS)
                        al = alpha[:, :, bass.ds(tile0, G)].rearrange("p h t -> p t h").unsqueeze(3)
                        last = nc.vector.tensor_tensor(v, v, al.to_broadcast([P, G, HEADS, HD]), ALU.mult)
                    last.then_inc(self.ind_built.sem, 1)

                for lo, hi, slots, skip in loops:
                    with dve.Fori(lo, hi) as i:
                        if slots > NG:
                            build(i * slots, i * G, EARLY, self.early[:, bass.ds(i * G, G), :])
                        for g in range(NG):
                            build(skip + i * slots + slots - NG + g, early + i * U + g * G, g % 2,
                                  self.rows[:, g * G:(g + 1) * G, :], (g, i))
                for n in range(late):
                    build(both + iters * NG + n, (both + n) * G, EARLY if n % 2 == 0 else 0,
                          self.early[:, (both + n) * G:(both + n + 1) * G, :])

            @block.tensor
            def _(pe):
                with ExitStack() as st:
                    regs = [st.enter_context(nc.tensor.register(f"window{n}_{self.names}")) for n in range(2 * G if extra else G)]

                    def total(n, tile0, buffer, rows, ring=None):
                        self._bases(pe, tile0, regs, extra)
                        pe.wait_ge(self.ind_built.sem, built0 + 1 + n)
                        if ring:
                            g, i = ring
                            pe.wait_ge(self.gathered[g].sem, gathered0 + (i + 1) * 16 * G)
                        self._accumulate(pe, tile0, buffer, regs, rows, extra)

                    if early:
                        pe.wait_ge(self.rows_moved.sem, self.rows_moved.at)
                    for lo, hi, slots, skip in loops:
                        with pe.Fori(lo, hi) as i:
                            if slots > NG:
                                total(i * slots, i * G, EARLY, [self.early[:, bass.ds(i * G + k, 1), :] for k in range(G)])
                            for g in range(NG):
                                total(skip + i * slots + slots - NG + g, early + i * U + g * G, g % 2,
                                      [self.rows[:, g * G + k, :] for k in range(G)], (g, i))
                    for n in range(late):
                        total(both + iters * NG + n, (both + n) * G, EARLY if n % 2 == 0 else 0,
                              [self.early[:, (both + n) * G + k, :] for k in range(G)])
        self.tiles_summed.up(NG * iters + early // G)
        self.ind_built.up(NG * iters + early // G)
        for g in range(NG):
            self.gathered[g].up(16 * G * iters)

    def max_pass(self, table):
        with self.scope():
            self._ring()
            self.ind = self.sb("ind", [P, 2, G, 2 * P])
            self.scan = self.sb("scan", [P, 2, G * P])
            self.back = self.sb("back", [P, 2, G, D])
            self.mask = self.sb("mask", [P, NG, G * P], BF16)
            self._max_pass(table)

    def _max_pass(self, table):
        nc, ps = self.nc, self.ps
        self.clear_accumulator()
        self.load_bases(PARTS)
        scan, back = self.scan, self.back

        @self.dve_steps
        def _(link):
            link(nc.vector.memset(scan[:], -BIG))
        extra = (self.dst3, PARTS)
        summed0, built0, gathered0, mask0 = self.tiles_summed.at, self.ind_built.at, self.gathered[0].at, self.mask_in[0].at
        turned0, scanned0, out0, drained0 = self.rows_turned.at, self.scanned.at, self.scan_turned.at, self.turned_out.at
        with nc.Block() as block:
            freed = Signal(self.rows_turned.sem)
            freed.at = turned0
            self._gathers(block, table, freed)

            @block.sync
            def _(sp):
                with sp.Fori(0, ITERS) as i:
                    for g in range(NG):
                        sp.wait_ge(self.scanned.sem, scanned0 + i * NG + g + 1)
                        sp.dma_start(self.mask[:, g, :], self.neg_d.rearrange("(a n) -> a n", a=1)[
                            :, bass.ds(i * (U * P) + g * G * P, G * P)].to_broadcast([P, G * P])).then_inc(self.mask_in[g].sem, 16)

            @block.vector
            def _(dve):
                dve.sem_inc(self.rows_turned.sem, NG)
                dve.sem_inc(self.scanned.sem, NG)
                dve.sem_inc(self.turned_out.sem, 1)
                dve.sem_inc(self.tiles_summed.sem, 2)
                with dve.Fori(0, ITERS) as i:
                    for g in range(NG):
                        dve.wait_ge(self.tiles_summed.sem, summed0 + 1 + i * NG + g)
                        for k in range(G):
                            col = bass.ds(i * U + g * G + k, 1)
                            last = nc.vector.tensor_scalar(self.ind[:, g % 2, k, :], self.iota_w[:], self.rel_a[:, col],
                                                           self.end_a[:, col], ALU.is_equal, ALU.mult)
                        last.then_inc(self.ind_built.sem, 1)
                        dve.wait_ge(self.rows_turned.sem, turned0 + NG + 1 + i * NG + g)
                        dve.wait_ge(self.mask_in[g].sem, mask0 + (i + 1) * 16)
                        dve.wait_ge(self.scanned.sem, scanned0 + NG + i * NG + g)
                        nc.vector.tensor_tensor_scan(
                            out=scan[:, g % 2, :], data0=self.mask[:, g, :], data1=ps[:, TURN:TURN + G * P],
                            initial=scan[:, (g + 1) % 2, G * P - 1:G * P], op0=ALU.add, op1=ALU.max).then_inc(self.scanned.sem, 1)

            @block.scalar
            def _(sc):
                with sc.Fori(0, ITERS) as i:
                    for g in range(NG):
                        sc.wait_ge(self.scan_turned.sem, out0 + 1 + i * NG + g)
                        sc.wait_ge(self.tiles_summed.sem, summed0 + 1 + i * NG + g)
                        nc.scalar.copy(back[:, g % 2], ps[:, TURN:TURN + G * P].rearrange(
                            "p (t f) -> p t f", t=G)).then_inc(self.turned_out.sem, 1)

            @block.tensor
            def _(pe):
                with ExitStack() as st:
                    regs = [st.enter_context(nc.tensor.register(f"window{n}_{self.names}")) for n in range(2 * G)]

                    def turn_in(i, g):
                        pe.wait_ge(self.gathered[g].sem, gathered0 + (i + 1) * 16 * G)
                        pe.wait_ge(self.turned_out.sem, drained0 + 1 + i * NG + g)
                        for k in range(G):
                            last = nc.tensor.transpose(ps[:, TURN + k * P:TURN + (k + 1) * P], self.rows[:, g * G + k, :], self.ident[:])
                        last.then_inc(self.rows_turned.sem, 1)

                    def turn_back(i, g):
                        pe.wait_ge(self.scanned.sem, scanned0 + NG + 1 + i * NG + g)
                        for k in range(G):
                            last = nc.tensor.transpose(ps[:, TURN + k * P:TURN + (k + 1) * P], scan[:, g % 2, k * P:(k + 1) * P], self.ident[:])
                        last.then_inc(self.scan_turned.sem, 1)

                    def sum_half(i, g, half):
                        if half == 0:
                            self._bases(pe, i * U + g * G, regs, extra)
                            pe.wait_ge(self.turned_out.sem, drained0 + 2 + i * NG + g)
                            pe.wait_ge(self.ind_built.sem, built0 + 1 + i * NG + g)
                        self._accumulate(pe, i * U + g * G, g % 2, regs, [back[:, g % 2, k, :] for k in range(G)], extra,
                                         range(2 * half, 2 * half + 2))

                    def groups(i, first):
                        for g in range(NG):
                            before = None if first and g == 0 else (i, g - 1) if g else (i - 1, NG - 1)
                            turn_in(i, g)
                            if before:
                                sum_half(*before, 0)
                            turn_back(i, g)
                            if before:
                                sum_half(*before, 1)

                    groups(0, True)
                    with pe.Fori(1, ITERS) as i:
                        groups(i, False)
                    sum_half(ITERS - 1, NG - 1, 0)
                    sum_half(ITERS - 1, NG - 1, 1)
        q = NG * ITERS
        self.rows_turned.up(NG + q)
        self.scanned.up(NG + q)
        self.turned_out.up(1 + q)
        self.scan_turned.up(q)
        self.tiles_summed.up(2 + q)
        self.ind_built.up(q)
        for g in range(NG):
            self.gathered[g].up(16 * G * ITERS)
            self.mask_in[g].up(16 * ITERS)

    def rank_nodes(self):
        nc, ps = self.nc, self.ps
        node = self.sb("node", [P, NT])
        none = self.sb("none", [P, NT])
        v = nc.vector

        @self.dve_steps
        def _(link):
            link(v.tensor_reduce(node[:], ps[:, EXTRA:EXTRA + NT * PARTS].rearrange("p (i s) -> p i s", s=PARTS), AX_X, ALU.add))
            link(v.tensor_scalar(none[:], node[:], 0.5, float(FARIDX), ALU.is_lt, ALU.mult))
            link(v.tensor_scalar(node[:], node[:], -1.0, None, ALU.add))
            link(v.tensor_tensor(self.node_i[:], node[:], none[:], ALU.add))

    def to_nodes(self, dram, to, width=D):
        nc, ps = self.nc, self.ps
        with self.scope():
            self._to_nodes(dram, self.sb("by_rank", [P, NT, D + HEADS]), width)
        self.load([(to, dram.rearrange("(i p) f -> p i f", p=P))])

    def _to_nodes(self, dram, out, width):
        nc, ps = self.nc, self.ps
        with nc.Block() as block:
            @block.vector
            def _(dve):
                for b in range(NBANK):
                    lo, hi = bank(b)
                    nc.vector.tensor_copy(out[:, lo // D:hi // D, 0:D], ps[:, lo:hi].rearrange("p (i f) -> p i f", f=D)).then_inc(self.dve_done.sem, 1)
                    self.dve_done.up()
                if width > D:
                    nc.vector.tensor_reduce(out[:, :, D:width], ps[:, EXTRA:EXTRA + NT * PARTS * (width - D)].rearrange(
                        "p (i s f) -> p i f s", i=NT, s=PARTS), AX_X, ALU.add).then_inc(self.dve_done.sem, 1)
                    self.dve_done.up()

            @block.gpsimd
            def _(pool):
                pool.wait_ge(self.dve_done.sem, self.dve_done.at)
                for i in range(NT):
                    nc.gpsimd.indirect_dma_start(
                        out=dram, out_offset=bass.IndirectOffsetOnAxis(ap=self.node_i[:, i:i + 1], axis=0),
                        in_=out[:, i, 0:width], in_offset=None, bounds_check=NP - 1, oob_is_err=False,
                    ).then_inc(self.stored.sem, 16)
                    self.stored.up(16)
                pool.wait_ge(self.stored.sem, self.stored.at)

    def edge_logits(self, u, v_nodes, ku, kv, table, early):
        with self.scope():
            sb = self.sb
            self.lo_b, self.rel_b = sb("lo_b", [P, 2, H8 * P], BF16), sb("rel_b", [P, 2, H8 * P], BF16)
            self.lo_hot, self.rel_hot = sb("lo_hot", [P, 2, H8 * P], BF16), sb("rel_hot", [P, 2, 2, H8 * P], BF16)
            self.hi_mask = sb("hi_mask", [P, 2, H8, NT], BF16)
            self.prod = sb("prod", [P, 2, H8 * ku * NT])
            self.us, self.vs = sb("us", [P, 2, H8, HEADS]), sb("vs", [P, 2, H8, 2 * HEADS])
            self._edge_logits(u, v_nodes, ku, kv, table, early)

    def _edge_logits(self, u, v_nodes, ku, kv, table, early):
        nc, ps = self.nc, self.ps
        v = nc.vector
        self.load_bases(PARTS * kv)
        vtab = self.dram(f"vtab{self.names}", [NP, 2 * HEADS])
        self.names += 1
        self.load([(vtab.rearrange("(i p) k -> p i k", p=P), v_nodes)])
        v_rank = self.v_rank
        vr = v_rank[:, :, 0:kv]

        @self.dve_steps
        def _(link):
            link(v.memset(v_rank[:], 0.0))
        with nc.Block() as block:
            @block.gpsimd
            def _(pool):
                for i in range(NT):
                    nc.gpsimd.indirect_dma_start(
                        out=v_rank[:, i, :], out_offset=None, in_=vtab, bounds_check=NP - 1, oob_is_err=False,
                        in_offset=bass.IndirectOffsetOnAxis(ap=self.node_i[:, i:i + 1], axis=0)).then_inc(self.stored.sem, 16)
                    self.stored.up(16)
                pool.wait_ge(self.stored.sem, self.stored.at)

        u3 = self.u3[:, :, 0:ku, :]
        v3 = self.v3[:, 0:NT * 3 * kv].rearrange("p (i s k) -> p s i k", s=3, k=kv)

        @self.dve_steps
        def _(link):
            self.split(link, u, [u3[:, n] for n in range(3)], self.rest[:, 0:ku * NT].rearrange("p (k i) -> p k i", k=ku))
            self.split(link, vr, [v3[:, n] for n in range(3)], self.rest[:, 0:NT * kv].rearrange("p (i k) -> p i k", k=kv))

        hot0, picked0, read0 = self.hot_built.at, self.picked.at, self.pick_read.at
        lo0, rel0 = self.lo_in[0].at, self.rel_in[0].at
        W = H8 * P
        row = lambda t, i, h: t.rearrange("(a n) -> a n", a=1)[:, bass.ds(i * (U * P) + h * W, W)].to_broadcast([P, W])
        with nc.Block() as block:
            self._prefetch(block, table, early)

            @block.sync
            def _(sp):
                with sp.Fori(0, ITERS) as i:
                    for h in range(2):
                        sp.wait_ge(self.hot_built.sem, hot0 + 1 + i * 2 + h)
                        sp.dma_start(self.lo_b[:, h, :], row(self.lo_d, i, h)).then_inc(self.lo_in[h].sem, 16)
                        sp.dma_start(self.rel_b[:, h, :], row(self.rel_d, i, h)).then_inc(self.rel_in[h].sem, 16)

            @block.tensor
            def _(pe):
                with ExitStack() as st:
                    regs = [st.enter_context(nc.tensor.register(f"window{n}_{self.names}")) for n in range(H8)]
                    with pe.Fori(0, ITERS) as i:
                        for h in range(2):
                            pe.load(regs, self.base[0:1, 1, bass.ds(i * U + h * H8, H8)])
                            pe.wait_ge(self.hot_built.sem, hot0 + 3 + i * 2 + h)
                            pe.wait_ge(self.pick_read.sem, read0 + 1 + i * 2 + h)
                            for k in range(H8):
                                c = slice(k * P, (k + 1) * P)
                                at = h * 2 * BANK + k * P
                                for n in range(3):
                                    nc.tensor.matmul(ps[:, at:at + ku * NT], self.lo_hot[:, h, c],
                                                     u3[:, n].rearrange("p k i -> p (k i)"), start=n == 0, stop=n == 2)
                                w = pe.snap(regs[k], min_val=0, max_val=(LASTB // P) * 3 * kv)
                                at = (4 + h) * BANK + k * 3 * kv
                                for half in range(2):
                                    last = nc.tensor.matmul(ps[:, at:at + 3 * kv], self.rel_hot[:, h, half, c],
                                                            self.v3[:, bass.ds(w + half * 3 * kv, 3 * kv)],
                                                            start=half == 0, stop=half == 1)
                            last.then_inc(self.picked.sem, 1)

            @block.vector
            def _(dve):
                dve.sem_inc(self.hot_built.sem, 2)
                dve.sem_inc(self.picked.sem, 2)
                dve.sem_inc(self.pick_read.sem, 2)

                def build(i, h):
                    dve.wait_ge(self.lo_in[h].sem, lo0 + (i + 1) * 16)
                    dve.wait_ge(self.rel_in[h].sem, rel0 + (i + 1) * 16)
                    dve.wait_ge(self.picked.sem, picked0 + 1 + i * 2 + h)
                    v.tensor_scalar(self.lo_hot[:, h, :], self.lo_b[:, h, :], self.iota_p[:, 0:1], None, ALU.is_equal)
                    for half in range(2):
                        v.tensor_scalar(self.rel_hot[:, h, half, :], self.rel_b[:, h, :], self.iota_p[:, half:half + 1], None, ALU.is_equal)
                    v.tensor_tensor(self.hi_mask[:, h], self.iota_h[:].unsqueeze(1).to_broadcast([P, H8, NT]),
                                    self.hi16_a[:, bass.ds(i * U + h * H8, H8)].unsqueeze(2).to_broadcast([P, H8, NT]),
                                    ALU.is_equal).then_inc(self.hot_built.sem, 1)

                def read(i, h):
                    chain0 = self.dve_chain.at
                    dve.wait_ge(self.picked.sem, picked0 + 3 + i * 2 + h)
                    lo = ps[:, h * 2 * BANK:(h + 1) * 2 * BANK].rearrange("p (t c) -> p t c", c=P)[:, :, 0:ku * NT]
                    hi = ps[:, (4 + h) * BANK:(4 + h) * BANK + H8 * 3 * kv].rearrange("p (t s k) -> p t k s", s=3, k=kv)
                    prod = self.prod[:, h, 0:H8 * ku * NT].rearrange("p (t k i) -> p t k i", t=H8, k=ku)
                    us, vs = self.us[:, h, :, 0:ku], self.vs[:, h, :, 0:kv]
                    at = bass.ds(i * U + h * H8, H8)
                    v.tensor_tensor(prod, lo.rearrange("p t (k i) -> p t k i", k=ku),
                                    self.hi_mask[:, h].unsqueeze(2).to_broadcast([P, H8, ku, NT]), ALU.mult).then_inc(self.dve_chain.sem, 1)
                    v.tensor_reduce(vs, hi, AX_X, ALU.add).then_inc(self.dve_chain.sem, 1)
                    dve.wait_ge(self.dve_chain.sem, chain0 + 1 + 3 * (i * 2 + h))
                    v.tensor_reduce(us, prod, AX_X, ALU.add).then_inc(self.dve_chain.sem, 1)
                    dve.wait_ge(self.dve_chain.sem, chain0 + 3 + 3 * (i * 2 + h))
                    last = v.tensor_tensor(self.lg_a[:, 0:ku, at], us.rearrange("p t k -> p k t"),
                                           vs[:, :, 0:ku].rearrange("p t k -> p k t"), ALU.add)
                    if kv > ku:
                        last = v.tensor_copy(self.self_a[:, :, at], vs[:, :, ku:].rearrange("p t k -> p k t"))
                    last.then_inc(self.pick_read.sem, 1)

                build(0, 0)
                with dve.Fori(0, ITERS - 1) as i:
                    build(i, 1)
                    read(i, 0)
                    build(i + 1, 0)
                    read(i, 1)
                build(ITERS - 1, 1)
                read(ITERS - 1, 0)
                read(ITERS - 1, 1)
        q = 2 * ITERS
        self.hot_built.up(2 + q)
        self.picked.up(2 + q)
        self.pick_read.up(2 + q)
        self.dve_chain.up(3 * q)
        for h in range(2):
            self.lo_in[h].up(16 * ITERS)
            self.rel_in[h].up(16 * ITERS)

    def _carries(self, f, g, k, maximum):
        nc, ps = self.nc, self.ps
        turned = self.pe_done.at
        init = -BIG if maximum else 0.0
        op0, op1 = (ALU.add, ALU.max) if maximum else (ALU.mult, ALU.add)
        cut = lambda n: self.cut_row[0:k, (2 if maximum else 0) + n, :]
        c = self.carry_row
        scanned = self.dve_done.at + 1
        with nc.Block() as block:
            @block.tensor
            def _(pe):
                nc.tensor.matmul(ps[0:k, 0:P], f[:, 0:k, J - 1], self.ident[:], start=True, stop=True)
                nc.tensor.matmul(ps[0:k, BANK:BANK + P], g[:, 0:k, 0], self.ident[:], start=True, stop=True).then_inc(self.pe_done.sem, 1)
                pe.wait_ge(self.dve_done.sem, scanned)
                nc.tensor.matmul(ps[:, 2 * BANK:2 * BANK + k], c[0:k, 0, 0:P], self.ident[0:k, 0:k], start=True, stop=True)
                nc.tensor.matmul(ps[:, 3 * BANK:3 * BANK + k], c[0:k, 1, 1:P + 1], self.ident[0:k, 0:k],
                                 start=True, stop=True).then_inc(self.pe_done.sem, 1)
                self.pe_done.up(2)

            @block.vector
            def _(dve):
                self.link(dve, nc.vector.memset(c[:], init))
                dve.wait_ge(self.pe_done.sem, turned + 1)
                nc.vector.tensor_tensor_scan(out=c[0:k, 0, 1:P + 1], data0=cut(0), data1=ps[0:k, 0:P], initial=init, op0=op0, op1=op1)
                nc.vector.tensor_tensor_scan(out=c[0:k, 1, 0:P][:, ::-1], data0=cut(1)[:, ::-1], data1=ps[0:k, BANK:BANK + P][:, ::-1],
                                             initial=init, op0=op0, op1=op1).then_inc(self.dve_done.sem, 1)
                self.dve_done.up()
                dve.wait_ge(self.pe_done.sem, turned + 2)
                self.link(dve, nc.vector.tensor_copy(self.carry[:, 0, 0:k], ps[:, 2 * BANK:2 * BANK + k]))
                self.link(dve, nc.vector.tensor_copy(self.carry[:, 1, 0:k], ps[:, 3 * BANK:3 * BANK + k]))

    def segment_softmax(self, k, slope, dist=None, own=False):
        nc, v, b = self.nc, self.nc.vector, self.b
        q = 2 * k if own else k
        qs = [self.lg_a[:, n, :] for n in range(k)] + [self.self_a[:, n, :] for n in range(k) if own]
        lg_d = self.dram(f"lg_d{self.names}", [q, EP])
        al_d = self.dram(f"al_d{self.names}", [q, EP])
        self.names += 1
        by_b = lambda t, n: t[n].rearrange("(p j) -> p j", p=P)
        by_c = lambda t, n: t[n].rearrange("(c t e) -> t c e", c=CH, t=CT)
        with self.scope():
            val_c = self.sb("val_c", [CT, q, CH, P])
            self.a_to_c([(val_c[:, n], qs[n]) for n in range(q)])
            self.load([(by_c(lg_d, n), val_c[:, n]) for n in range(q)])
        with self.scope():
            self.l_b = self.sb("l_b", [P, q, J])
            self.f_b, self.g_b, self.m_b = (self.sb(n, [P, k, J]) for n in ("f_b", "g_b", "m_b"))
            self._softmax_b(k, q, slope, dist, own, lg_d, al_d, by_b)
        with self.scope():
            val_c = self.sb("val_c", [CT, q, CH, P])
            self.load([(val_c[:, n], by_c(al_d, n)) for n in range(q)])
            self.c_to_a([(qs[n], val_c[:, n]) for n in range(q)])

    def _softmax_b(self, k, q, slope, dist, own, lg_d, al_d, by_b):
        nc, v, b = self.nc, self.nc.vector, self.b
        self.load([(self.l_b[:, n, :], by_b(lg_d, n)) for n in range(q)])
        l, f, g, m = self.l_b, self.f_b, self.g_b, self.m_b
        rev = lambda t: t[:, ::-1]

        def scans(link, kinds, op0, op1, init):
            for n in range(k):
                link(v.tensor_tensor_scan(out=f[:, n, :], data0=b[kinds[0]][:], data1=l[:, n, :],
                                          initial=init, op0=op0, op1=op1))
                link(v.tensor_tensor_scan(out=rev(g[:, n, :]), data0=rev(b[kinds[1]]), data1=rev(l[:, n, :]),
                                          initial=init, op0=op0, op1=op1))

        @self.dve_steps
        def _(link):
            if dist is not None:
                link(v.scalar_tensor_tensor(out=l[:, 0, :], in0=self.w1_b[:], scalar=dist, in1=l[:, 0, :],
                                            op0=ALU.mult, op1=ALU.add))
            link(v.scalar_tensor_tensor(out=l[:, 0:q, :], in0=l[:, 0:q, :], scalar=slope, in1=l[:, 0:q, :], op0=ALU.mult, op1=ALU.max))
            scans(link, ("neg_f", "neg_g"), ALU.add, ALU.max, -BIG)

        self._carries(f, g, k, True)

        @self.dve_steps
        def _(link):
            link(v.tensor_tensor(m[:, 0:k, :], f[:, 0:k, :], g[:, 0:k, :], ALU.max))
            for n in range(k):
                for d, cut in enumerate(("cut_f", "cut_g")):
                    link(v.scalar_tensor_tensor(out=m[:, n, :], in0=b[cut][:], scalar=self.carry[:, d, n:n + 1], in1=m[:, n, :],
                                                op0=ALU.add, op1=ALU.max))
            if own:
                link(v.tensor_tensor(m[:, 0:k, :], m[:, 0:k, :], l[:, k:q, :], ALU.max))
                link(v.tensor_tensor(l[:, k:q, :], l[:, k:q, :], m[:, 0:k, :], ALU.subtract))
            link(v.tensor_tensor(l[:, 0:k, :], l[:, 0:k, :], m[:, 0:k, :], ALU.subtract))

        with nc.Block() as block:
            @block.scalar
            def _(sc):
                nc.scalar.activation(l[:, 0:q, :], l[:, 0:q, :], ACT.Exp)

        @self.dve_steps
        def _(link):
            scans(link, ("go_f", "go_g"), ALU.mult, ALU.add, 0.0)

        self._carries(f, g, k, False)

        @self.dve_steps
        def _(link):
            link(v.tensor_tensor(m[:, 0:k, :], f[:, 0:k, :], g[:, 0:k, :], ALU.add))
            link(v.tensor_tensor(m[:, 0:k, :], m[:, 0:k, :], l[:, 0:k, :], ALU.subtract))
            for n in range(k):
                for d, open_ in enumerate(("open_f", "open_g")):
                    link(v.scalar_tensor_tensor(out=m[:, n, :], in0=b[open_][:], scalar=self.carry[:, d, n:n + 1], in1=m[:, n, :],
                                                op0=ALU.mult, op1=ALU.add))
            if own:
                link(v.tensor_tensor(m[:, 0:k, :], m[:, 0:k, :], l[:, k:q, :], ALU.add))
                link(v.tensor_scalar(m[:, 0:k, :], m[:, 0:k, :], 1e-16, None, ALU.add))
            link(v.reciprocal(m[:, 0:k, :], m[:, 0:k, :]))
            link(v.tensor_tensor(l[:, 0:k, :], l[:, 0:k, :], m[:, 0:k, :], ALU.mult))
            if own:
                link(v.tensor_tensor(l[:, k:q, :], l[:, k:q, :], m[:, 0:k, :], ALU.mult))

        self.load([(by_b(al_d, n), l[:, n, :]) for n in range(q)])

    def store_table(self, rows):
        self.load([(self.table.rearrange("(i p) f -> p i f", p=P), rows[:].rearrange("p (i f) -> p i f", f=D))])

    def matrices(self, *names):
        return [self.sb(n, [P, D]) for n in names]

    def nodes(self, *names):
        return [self.sb(n, [P, NP]) for n in names]

    def run(self):
        self.constants()
        self.stat = self.sb("stat", [P, 6, NT])
        self.node_i = self.sb("node_i", [P, NT], I32)
        self.y, self.z = self.nodes("y", "z")
        self.table, self.kept = self.dram("table", [NP, D]), self.dram("kept", [NP, D])
        kept = self.kept.rearrange("(i p) f -> p i f", p=P)
        with self.scope():
            self.edge_lists()
        self.edge_structure()
        with self.scope():
            self.x, = self.nodes("x")
            self.layer_of_maxima()
            self.layer_of_sums()

            @self.dve_steps
            def _(link):
                link(self.nc.vector.tensor_copy(self.z[:], self.x[:]))

            self.load([(kept, rows_view(self.x))])
        with self.scope():
            self.attention_buffers()
            self.layer_of_attention()
            self.layer_of_heads()
        view, x = rows_view, self.z
        self.load([(self.out[0:(NT - 1) * P, :].rearrange("(i p) f -> p i f", p=P), view(x)[:, 0:NT - 1, :]),
                   (self.out[(NT - 1) * P:N, :], view(x)[0:TAIL, NT - 1, :])])

    def layer_of_maxima(self):
        a, v, x, y, z, view = self.a, self.nc.vector, self.x, self.y, self.z, rows_view
        with self.scope():
            t1, h_t, t3 = self.nodes("t1", "h_t", "t3")
            w_in, w_up1, w_up2, w_out, g1, be1, g2, be2 = self.matrices("w_in", "w_up1", "w_up2", "w_out", "g1", "be1", "g2", "be2")
            ffn1, ffn2, ffn1_b = self.sb("ffn1", [P, 4 * D]), self.sb("ffn2", [P, 4, D]), self.sb("ffn1_b", [P, 4])
            b_in, b_up, b_out, b_ffn2 = (self.sb(n, [P, 1]) for n in ("b_in", "b_up", "b_out", "b_ffn2"))

            @self.dve_steps
            def _(link):
                link(v.memset(x[:], 0.0))
            with self.nc.allow_non_contiguous_dma(reason="biases of 128 values as columns"):
                self.load([
                    (view(x)[:, 0:NT - 1, :], a["x"][0:(NT - 1) * P, :].rearrange("(i p) f -> p i f", p=P)),
                    (view(x)[0:TAIL, NT - 1, :], a["x"][(NT - 1) * P:N, :]),
                    (w_in[:], a["L0_gnn_W_in_w"]), (w_up1[:], a["L0_gnn_W_upd_w"][0:D, :]), (w_up2[:], a["L0_gnn_W_upd_w"][D:, :]),
                    (w_out[:], a["L0_gnn_W_out_w"]), (g1[:], on_all(a["L0_gnn_ln1_g"])), (be1[:], on_all(a["L0_gnn_ln1_b"])),
                    (g2[:], on_all(a["L0_gnn_ln2_g"])), (be2[:], on_all(a["L0_gnn_ln2_b"])),
                    (ffn1[:], a["L0_gnn_ffn1_w"]), (ffn2[:], a["L0_gnn_ffn2_w"].rearrange("(c k) f -> k c f", k=P)),
                    (b_in[:], column(a["L0_gnn_W_in_b"])), (b_up[:], column(a["L0_gnn_W_upd_b"])),
                    (b_out[:], column(a["L0_gnn_W_out_b"])), (b_ffn2[:], column(a["L0_gnn_ffn2_b"])),
                    (ffn1_b[:], a["L0_gnn_ffn1_b"].rearrange("(c k) -> k c", k=P)),
                ])
            self.turn(t1, x)
            self.linear_t(h_t, [(w_in[:], t1)], b_in[:])
            self.turn(y, h_t)
            self.store_table(y)
            self.max_pass(self.table)
            self.rank_nodes()
            with self.scope():
                agg = self.sb("agg", [P, NT, D])
                self.to_nodes(self.agg_max, agg[:])

                @self.dve_steps
                def _(link):
                    link(v.tensor_tensor(view(y), agg[:], view(y), ALU.subtract))
                    link(v.scalar_tensor_tensor(out=view(y), in0=agg[:], scalar=LOWEST / 3, in1=view(y),
                                                op0=ALU.is_gt, op1=ALU.mult))
            self.turn(t1, y)
            self.linear_t(t3, [(w_up1[:], h_t), (w_up2[:], t1)], b_up[:])
            self.linear_t(h_t, [(w_out[:], t3)], b_out[:])
            self.turn(y, h_t, add=x)
            self.layer_norm(y, y, 1e-5, g1, be1)
            self.turn(t1, y)
            with self.scope():
                hidden = [h_t, t3, z, *self.nodes("t4")]
                for c in range(4):
                    self.linear_t(hidden[c], [(ffn1[:, c * D:(c + 1) * D], t1)], ffn1_b[:, c:c + 1], gelu=True)
                self.linear_t(t1, [(ffn2[:, c, :], hidden[c]) for c in range(4)], b_ffn2[:])
            self.turn(z, t1, add=y)
            self.layer_norm(z, z, 1e-5, g2, be2)

        @self.dve_steps
        def _(link):
            link(v.tensor_tensor(x[:], x[:], z[:], ALU.add))
        self.layer_norm(x, x, 1e-5)

    def layer_of_sums(self):
        nc, a, v, x, y, z, view, st = self.nc, self.a, self.nc.vector, self.x, self.y, self.z, rows_view, self.stat
        self.store_table(x)
        with self.scope():
            self._ring()
            self.sum_pass(self.table, self.w_a[:].unsqueeze(1))
        with self.scope():
            t1, t2, t3 = self.nodes("t1", "t2", "t3")
            w1, w2 = self.matrices("w1", "w2")
            b1, b2, b = (self.sb(n, [P, 1]) for n in ("b1", "b2", "b"))
            agg = self.sb("agg", [P, NT, D])
            with nc.allow_non_contiguous_dma(reason="biases of 128 values as columns"):
                self.load([(w1[:], a["L1_gnn_W1"]), (w2[:], a["L1_gnn_W2"]),
                           (b1[:], a["L1_gnn_b1"].rearrange("o n -> n o")), (b2[:], a["L1_gnn_b2"].rearrange("o n -> n o"))])
            self.to_nodes(self.agg, agg[:])

            @self.dve_steps
            def _(link):
                link(v.tensor_tensor(view(y), agg[:], view(x), ALU.add))
                link(v.tensor_tensor(view(z), agg[:], view(x), ALU.mult))
                link(v.tensor_tensor(b[:], b1[:], b2[:], ALU.add))
            self.turn(t1, y)
            self.turn(t2, z)
            self.linear_t(t3, [(w1[:], t1), (w2[:], t2)], b[:])
            self.turn(y, t3)

        @self.dve_steps
        def _(link):
            link(v.scalar_tensor_tensor(out=y[:], in0=y[:], scalar=0.2, in1=y[:], op0=ALU.mult, op1=ALU.max))
            link(v.tensor_tensor(z[:], y[:], y[:], ALU.mult))
            link(v.tensor_reduce(st[:, 0, :], view(z), AX_X, ALU.add))
        with nc.Block() as block:
            @block.scalar
            def _(sc):
                nc.scalar.activation(st[:, 1, :], st[:, 0, :], ACT.Sqrt)

        @self.dve_steps
        def _(link):
            link(v.tensor_scalar(st[:, 1, :], st[:, 1, :], 1e-12, None, ALU.max))
            link(v.reciprocal(st[:, 2, :], st[:, 1, :]))
            link(v.tensor_tensor(view(y), view(y), st[:, 2, :].unsqueeze(2).to_broadcast([P, NT, D]), ALU.mult))
            link(v.tensor_tensor(x[:], x[:], y[:], ALU.add))
        self.layer_norm(x, x, 1e-5)

    def attention_buffers(self):
        sb = self.sb
        self.u3 = sb("u3", [P, 3, HEADS, NT], BF16)
        self.v3 = sb("v3", [P, NT * 3 * 2 * HEADS], BF16)
        self.v_rank = sb("v_rank", [P, NT, 2 * HEADS])
        self.rest = sb("rest", [P, NT * 2 * HEADS])
        self.carry_row = sb("carry_row", [HEADS, 2, P + 1])
        self.carry = sb("carry", [P, 2, HEADS])
        self.att = sb("att", [P, 2 * HEADS])
        self.uv = sb("uv", [P, NT, 2 * HEADS])
        self.u_n = sb("u_n", [P, HEADS, NT])
        self.v_n = sb("v_n", [P, NT, 2 * HEADS])

    def layer_of_attention(self):
        a, v, y, z, view, att = self.a, self.nc.vector, self.y, self.z, rows_view, self.att
        uv, u_n, v_n = self.uv, self.u_n, self.v_n
        dist = self.sb("dist", [P, 3])

        @self.dve_steps
        def _(link):
            link(v.memset(v_n[:], 0.0))
        for r in range(3):
            with self.scope():
                t1, t2 = self.nodes("t1", "t2")
                w1, w2 = self.matrices("w1", "w2")
                self.load([(w1[:], a["L2_gnn_W1"][r]), (w2[:], a["L2_gnn_W2"][r]),
                           (att[:, 0:1], a["L2_gnn_Wa"][r, 0:D, :]), (att[:, 1:2], a["L2_gnn_Wa"][r, D:2 * D, :]),
                           (dist[:, 0:1], a["L2_gnn_W0"][r].to_broadcast([P, 1])),
                           (dist[:, 1:2], a["L2_gnn_Wa"][r, 2 * D:, :].to_broadcast([P, 1]))])
                self.turn(t1, z)
                self.linear_t(t2, [(w1[:], t1)])
                self.linear_rows(view(y), t1, w1[:], D)
                self.store_table(y)
                self.linear_rows(uv[:, :, 0:2], t2, att[:, 0:2], 2)
                self.linear_rows(view(z), t1, w2[:], D)

            @self.dve_steps
            def _(link):
                link(v.tensor_copy(u_n[:, 0:1, :], uv[:, :, 0:1].rearrange("p i k -> p k i")))
                link(v.tensor_copy(v_n[:, :, 0:1], uv[:, :, 1:2]))
                link(v.tensor_tensor(dist[:, 2:3], dist[:, 0:1], dist[:, 1:2], ALU.mult))
            with self.scope():
                early = 160
                self.lg_a = self.sb("lg_a", [P, 1, TILES])
                self._ring()
                self.early = self.sb("early", [P, early, D])
                self.edge_logits(u_n[:, 0:1, :], v_n[:], 1, 1, self.table, early)
                self.segment_softmax(1, 0.01, dist=dist[:, 2:3])
                self.sum_pass(self.table, self.lg_a, early=early)
            with self.scope():
                agg = self.sb("agg", [P, NT, D])
                self.to_nodes(self.agg, agg[:])

                @self.dve_steps
                def _(link):
                    link(v.tensor_tensor(view(z), view(z), agg[:], ALU.add))
                    link(v.tensor_scalar(z[:], z[:], 0.0, None, ALU.max))

        kept = self.kept.rearrange("(i p) f -> p i f", p=P)
        self.load([(view(y), kept)])

        @self.dve_steps
        def _(link):
            link(v.tensor_tensor(z[:], y[:], z[:], ALU.add))
        self.layer_norm(z, z, 1e-5)
        self.load([(kept, view(z))])

    def layer_of_heads(self):
        a, v, y, z, view, att = self.a, self.nc.vector, self.y, self.z, rows_view, self.att
        uv, u_n, v_n = self.uv, self.u_n, self.v_n
        gamma, beta, bias = self.matrices("gamma", "beta", "bias")
        with self.scope():
            t1, t2 = self.nodes("t1", "t2")
            w, = self.matrices("w")

            @self.dve_steps
            def _(link):
                link(v.memset(att[:], 0.0))
            with self.nc.allow_non_contiguous_dma(reason="256 attention weights as columns"):
                self.load([(w[:], a["L3_gnn_W"]), (gamma[:], on_all(a["L3_gnn_gamma"])), (beta[:], on_all(a["L3_gnn_beta"])),
                           (bias[:], on_all(a["L3_gnn_bias"]))]
                          + [(att[h * HD:(h + 1) * HD, s * HEADS + h:s * HEADS + h + 1], column(a[n][0, h]))
                             for s, n in enumerate(("L3_gnn_att_src", "L3_gnn_att_dst")) for h in range(HEADS)])
            self.turn(t1, z)
            self.linear_t(t2, [(w[:], t1)])
            self.linear_rows(view(y), t1, w[:], D)
            self.store_table(y)
            self.linear_rows(uv[:], t2, att[:], 2 * HEADS)

        @self.dve_steps
        def _(link):
            link(v.tensor_copy(u_n[:], uv[:, :, 0:HEADS].rearrange("p i k -> p k i")))
            link(v.tensor_copy(v_n[:, :, 0:HEADS], uv[:, :, HEADS:]))
            link(v.tensor_tensor(v_n[:, :, HEADS:], uv[:, :, 0:HEADS], uv[:, :, HEADS:], ALU.add))
        with self.scope():
            early = 32
            self.lg_a = self.sb("lg_a", [P, HEADS, TILES])
            self.self_a = self.sb("self_a", [P, HEADS, TILES])
            self._ring()
            self.early = self.sb("early", [P, early, D])
            self.edge_logits(u_n[:], v_n[:], HEADS, 2 * HEADS, self.table, early)
            self.segment_softmax(HEADS, 0.2, own=True)

            @self.dve_steps
            def _(link):
                link(v.tensor_tensor(self.self_a[:], self.self_a[:], self.end_a[:].unsqueeze(1).to_broadcast([P, HEADS, TILES]), ALU.mult))
            with self.scope():
                self3 = self.sb("self3", [P, PARTS, HEADS, TILES], BF16)
                with self.scope():
                    rest = self.sb("rest", [P, HEADS, TILES])

                    @self.dve_steps
                    def _(link):
                        self.split(link, self.self_a[:], [self3[:, n] for n in range(PARTS)], rest[:])
                self.sum_pass(self.table, self.lg_a, heads=True, early=early,
                              extra=(self3[:].rearrange("p s k t -> p (s k) t"), PARTS * HEADS))
        with self.scope():
            agg = self.sb("agg", [P, NT, D + HEADS])
            self.to_nodes(self.agg3, agg[:], D + HEADS)

            @self.dve_steps
            def _(link):
                for h in range(HEADS):
                    link(v.tensor_tensor(view(y)[:, :, h * HD:(h + 1) * HD], view(y)[:, :, h * HD:(h + 1) * HD],
                                        agg[:, :, D + h:D + h + 1].to_broadcast([P, NT, HD]), ALU.mult))
                link(v.tensor_tensor(view(y), view(y), agg[:, :, 0:D], ALU.add))
                link(v.tensor_tensor(view(y), view(y), bias[:].unsqueeze(1).to_broadcast([P, NT, D]), ALU.add))
        self.layer_norm(y, y, 1e-5, gamma, beta)

        @self.dve_steps
        def _(link):
            link(v.tensor_scalar(y[:], y[:], 0.0, None, ALU.max))
            link(v.tensor_tensor(z[:], z[:], y[:], ALU.add))
        self.layer_norm(z, z, 1e-5)


def graph_layers(nc, args, out):
    with ExitStack() as ctx:
        Kernel(nc, ctx, args, out).run()


def kernel(**inputs):
    import concourse.bacc as bacc
    from concourse.bass_utils import run_bass_kernel_spmd

    nc = bacc.Bacc("TRN2", target_bir_lowering=False, num_devices=1)
    arrays, args = {}, {}
    for name, value in inputs.items():
        value = np.ascontiguousarray(value)
        arrays[f"in_{name}"] = value
        args[name] = nc.dram_tensor(f"in_{name}", value.shape, mybir.dt.from_np(value.dtype), kind="ExternalInput").ap()
    out = nc.dram_tensor("out_x", (N, D), F32, kind="ExternalOutput").ap()
    graph_layers(nc, args, out)
    result = run_bass_kernel_spmd(nc, [arrays], core_ids=[0])
    return result.results[0]["out_x"]
```

```python
from contextlib import ExitStack, contextmanager

import numpy as np

import concourse.bass as bass
from concourse import mybir
from concourse.alu_op_type import AluOpType as ALU

F32 = mybir.dt.float32
BF16 = mybir.dt.bfloat16
I32 = mybir.dt.int32
ACT = mybir.ActivationFunctionType
AX_X = mybir.AxisListType.X

P = 128
N = 3125
E = 100000
D = 128
HEADS, HD = 4, 32
NT = -(-N // P)
NP = NT * P
TAIL = N - (NT - 1) * P
U = 16
TILES = -(-E // (P * U)) * U
ITERS = TILES // U
EP = TILES * P
J = EP // P
CH = 7
CT = TILES // CH
LASTB = NP - 2 * P
BANK = 512
NBANK = -(-NP // BANK)
BIG = 1e30
LOWEST = -3.0e38
PADDST = 4095
FARIDX = 8192
G = 4
NG = U // G
PARTS = 3
EXTRA = NP
TURN = 7 * BANK
H8 = U // 2
AHEAD = 100


class Signal:

    def __init__(self, sem):
        self.sem, self.at = sem, 0

    def up(self, n=1):
        self.at += n
        return self.at


def rows_view(t):
    return t[:].rearrange("p (i f) -> p i f", f=D)


def column(t):
    return t.rearrange("(n o) -> n o", o=1)


def on_all(t):
    return t.rearrange("(o n) -> o n", o=1).to_broadcast([P, t.shape[0]])


def bank(b):
    return b * BANK, min(NP, (b + 1) * BANK)


class Kernel:
    def __init__(self, nc, ctx, args, out):
        self.nc, self.ctx, self.a, self.out = nc, ctx, args, out
        self.names = 0
        signal = lambda name: Signal(ctx.enter_context(nc.semaphore(name)))
        self.pe_done, self.dve_done = signal("pe_done"), signal("dve_done")
        self.act_done, self.pool_done = signal("act_done"), signal("pool_done")
        self.dve_chain = signal("dve_chain")
        self.loaded, self.stored = signal("loaded"), signal("stored")
        self.v_kept = signal("v_kept")
        self.idx_staged, self.group_begun = signal("idx_staged"), signal("group_begun")
        self.ind_built, self.tiles_summed = signal("ind_built"), signal("tiles_summed")
        self.rows_turned, self.scanned = signal("rows_turned"), signal("scanned")
        self.scan_turned, self.turned_out = signal("scan_turned"), signal("turned_out")
        self.hot_built, self.picked, self.pick_read = signal("hot_built"), signal("picked"), signal("pick_read")
        self.gathered = [Signal(ctx.enter_context(nc.semaphore(f"gathered{g}"))) for g in range(NG)]
        self.rows_kept = [Signal(ctx.enter_context(nc.semaphore(f"rows_kept{g}"))) for g in range(NG)]
        self.ahead_in = [Signal(ctx.enter_context(nc.semaphore(f"ahead_in{s}"))) for s in range(NG)]
        self.mask_in = [Signal(ctx.enter_context(nc.semaphore(f"mask_in{g}"))) for g in range(NG)]
        self.lo_in = [Signal(ctx.enter_context(nc.semaphore(f"lo_in{g}"))) for g in range(2)]
        self.rel_in = [Signal(ctx.enter_context(nc.semaphore(f"rel_in{g}"))) for g in range(2)]
        self.ps = ctx.enter_context(nc.psum_tensor("ps", [P, 8 * BANK], F32))

    def sb(self, name, shape, dt=F32):
        self.names += 1
        return self.ctx.enter_context(self.nc.sbuf_tensor(f"{name}_{self.names}", shape, dt))

    @contextmanager
    def scope(self):
        outer = self.ctx
        with ExitStack() as self.ctx:
            yield
        self.ctx = outer

    def dram(self, name, shape, dt=F32):
        return self.nc.dram_tensor(name, shape, dt, kind="Internal").ap()

    def link(self, eng, ins):
        eng_wait = self.dve_chain.up()
        ins.then_inc(self.dve_chain.sem, 1)
        eng.wait_ge(self.dve_chain.sem, eng_wait)

    def load(self, pairs, wait=True):
        with self.nc.Block() as block:
            @block.sync
            def _(sp):
                for to, of in pairs:
                    sp.dma_start(to, of).then_inc(self.loaded.sem, 16)
                    self.loaded.up(16)
                if wait:
                    sp.wait_ge(self.loaded.sem, self.loaded.at)

    def _drain_banks(self, block, ready, vec, act):
        @block.vector
        def _(dve):
            for b in range(NBANK):
                if b % 2 == 0 or act is None:
                    dve.wait_ge(self.pe_done.sem, ready[b])
                    vec(*bank(b)).then_inc(self.dve_done.sem, 1)
                    self.dve_done.up()
            dve.wait_ge(self.dve_done.sem, self.dve_done.at)

        @block.scalar
        def _(sc):
            if act is None:
                return
            for b in range(NBANK):
                if b % 2 == 1 or vec is None:
                    sc.wait_ge(self.pe_done.sem, ready[b])
                    act(*bank(b)).then_inc(self.act_done.sem, 1)
                    self.act_done.up()
            sc.wait_ge(self.act_done.sem, self.act_done.at)

    def turn(self, to, of, add=None):
        nc, ps = self.nc, self.ps
        ready = []
        with nc.Block() as block:
            @block.tensor
            def _(pe):
                for i in range(NT):
                    c = slice(i * P, (i + 1) * P)
                    nc.tensor.transpose(ps[:, c], of[:, c], self.ident[:]).then_inc(self.pe_done.sem, 1)
                    self.pe_done.up()
                    if i % 4 == 3 or i == NT - 1:
                        ready.append(self.pe_done.at)

            if add is None:
                self._drain_banks(block, ready,
                                  lambda a, b: nc.vector.tensor_copy(to[:, a:b], ps[:, a:b]),
                                  lambda a, b: nc.scalar.copy(to[:, a:b], ps[:, a:b]))
            else:
                self._drain_banks(block, ready,
                                  lambda a, b: nc.vector.tensor_tensor(to[:, a:b], ps[:, a:b], add[:, a:b], ALU.add),
                                  None)

    def linear_t(self, to, terms, bias=None, gelu=False):
        nc, ps = self.nc, self.ps
        ready = []
        with nc.Block() as block:
            @block.tensor
            def _(pe):
                for b in range(NBANK):
                    lo, hi = bank(b)
                    for n, (w, x) in enumerate(terms):
                        last = nc.tensor.matmul(ps[:, lo:hi], w, x[:, lo:hi], start=n == 0, stop=n == len(terms) - 1)
                    last.then_inc(self.pe_done.sem, 1)
                    ready.append(self.pe_done.up())

            if gelu:
                @block.scalar
                def _(sc):
                    for b in range(NBANK):
                        lo, hi = bank(b)
                        sc.wait_ge(self.pe_done.sem, ready[b])
                        nc.scalar.activation(to[:, lo:hi], ps[:, lo:hi], ACT.Gelu, bias=bias).then_inc(self.act_done.sem, 1)
                        self.act_done.up()
                    sc.wait_ge(self.act_done.sem, self.act_done.at)
            elif bias is None:
                self._drain_banks(block, ready,
                                  lambda a, b: nc.vector.tensor_copy(to[:, a:b], ps[:, a:b]),
                                  lambda a, b: nc.scalar.copy(to[:, a:b], ps[:, a:b]))
            else:
                self._drain_banks(block, ready,
                                  lambda a, b: nc.vector.tensor_scalar(to[:, a:b], ps[:, a:b], bias, None, ALU.add),
                                  lambda a, b: nc.scalar.activation(to[:, a:b], ps[:, a:b], ACT.Identity, bias=bias))

    def project(self, x_t, h_t, w, att, width, spread, w_own=None):
        nc, ps, y, z = self.nc, self.ps, rows_view(self.y), rows_view(self.z)
        pe0, dve0 = self.pe_done.at, self.dve_done.at
        uv_at = 7 * BANK
        tiles = lambda b: range(4 * b, min(4 * b + 4, NT))
        bank_rows = lambda b: ps[:, b * BANK:b * BANK + len(tiles(b)) * D].rearrange("p (i f) -> p i f", f=D)
        with nc.Block() as block:
            @block.tensor
            def _(pe):
                for i in range(NT):
                    last = nc.tensor.matmul(ps[:, uv_at + i * width:uv_at + (i + 1) * width], h_t[:, i * P:(i + 1) * P], att,
                                            start=True, stop=True)
                last.then_inc(self.pe_done.sem, 1)
                for n, matrix in enumerate((w, w_own) if w_own is not None else (w,)):
                    for b in range(NBANK):
                        if n:
                            pe.wait_ge(self.dve_done.sem, dve0 + 2 + b)
                        for i in tiles(b):
                            last = nc.tensor.matmul(ps[:, i * P:(i + 1) * P], x_t[:, i * P:(i + 1) * P], matrix, start=True, stop=True)
                        last.then_inc(self.pe_done.sem, 1)

            @block.vector
            def _(dve):
                self.link(dve, nc.vector.memset(self.v_rank[:], 0.0))
                dve.wait_ge(self.pe_done.sem, pe0 + 1)
                self.link(dve, nc.vector.tensor_copy(self.uv[:, :, 0:width], ps[:, uv_at:uv_at + NT * width].rearrange(
                    "p (i k) -> p i k", k=width)))
                spread(lambda ins: self.link(dve, ins))
                dve.sem_inc(self.dve_done.sem, 1)
                for b in range(NBANK):
                    dve.wait_ge(self.pe_done.sem, pe0 + 2 + b)
                    nc.vector.tensor_copy(y[:, 4 * b:4 * b + len(tiles(b)), :], bank_rows(b)).then_inc(self.dve_done.sem, 1)
                dve.wait_ge(self.dve_done.sem, dve0 + 1 + NBANK)

            if w_own is not None:
                @block.scalar
                def _(sc):
                    for b in range(NBANK):
                        sc.wait_ge(self.pe_done.sem, pe0 + 2 + NBANK + b)
                        nc.scalar.copy(z[:, 4 * b:4 * b + len(tiles(b)), :], bank_rows(b)).then_inc(self.act_done.sem, 1)
                        self.act_done.up()
                    sc.wait_ge(self.act_done.sem, self.act_done.at)

            self.v_kept.up(16)
            self.loaded.up(16)

            @block.sync
            def _(sp):
                sp.wait_ge(self.dve_done.sem, dve0 + 1)
                sp.dma_start(self.v_table.rearrange("(i p) k -> p i k", p=P), self.v_n[:]).then_inc(self.v_kept.sem, 16)
                sp.wait_ge(self.dve_done.sem, dve0 + 1 + NBANK)
                sp.dma_start(self.table.rearrange("(i p) f -> p i f", p=P), y).then_inc(self.loaded.sem, 16)
                sp.wait_ge(self.v_kept.sem, self.v_kept.at)
                sp.wait_ge(self.loaded.sem, self.loaded.at)

            @block.gpsimd
            def _(pool):
                pool.wait_ge(self.v_kept.sem, self.v_kept.at)
                for i in range(NT):
                    nc.gpsimd.indirect_dma_start(
                        out=self.v_rank[:, i, :], out_offset=None, in_=self.v_table, bounds_check=NP - 1, oob_is_err=False,
                        in_offset=bass.IndirectOffsetOnAxis(ap=self.node_i[:, i:i + 1], axis=0)).then_inc(self.stored.sem, 16)
                    self.stored.up(16)
                pool.wait_ge(self.stored.sem, self.stored.at)
        self.pe_done.up(1 + NBANK * (2 if w_own is not None else 1))
        self.dve_done.up(1 + NBANK)

    def layer_norm(self, to, x, eps, gamma=None, beta=None):
        nc, st = self.nc, self.stat
        row = lambda r: r[:].unsqueeze(1).to_broadcast([P, NT, D])
        mean, var, root, scale, half = (st[:, c, :] for c in range(5))
        with self.scope():
            stats = self.sb("stats", [P, NT, 6])
            with nc.Block() as block:
                @block.vector
                def _(dve):
                    for i in range(NT):
                        last = nc.vector.bn_stats(stats[:, i, :], rows_view(x)[:, i, :])
                    self.link(dve, last)
                    self.link(dve, nc.vector.tensor_tensor(mean, stats[:, :, 1], stats[:, :, 4], ALU.add))
                    self.link(dve, nc.vector.tensor_tensor(half, stats[:, :, 1], stats[:, :, 4], ALU.subtract))
                    self.link(dve, nc.vector.tensor_scalar(mean, mean, 0.5, None, ALU.mult))
                    self.link(dve, nc.vector.tensor_tensor(var, stats[:, :, 2], stats[:, :, 5], ALU.add))
                    self.link(dve, nc.vector.tensor_tensor(half, half, half, ALU.mult))
                    self.link(dve, nc.vector.tensor_scalar(half, half, 0.25, eps, ALU.mult, ALU.add))
                    nc.vector.scalar_tensor_tensor(out=var, in0=var, scalar=1.0 / D, in1=half, op0=ALU.mult,
                                                   op1=ALU.add).then_inc(self.dve_done.sem, 1)
                    self.dve_done.up()
                    dve.wait_ge(self.act_done.sem, self.act_done.at + 1)
                    self.link(dve, nc.vector.reciprocal(scale, root))
                    for i in range(NT):
                        last = nc.vector.tensor_scalar(rows_view(to)[:, i, :], rows_view(x)[:, i, :], mean[:, i:i + 1],
                                                       scale[:, i:i + 1], ALU.subtract, ALU.mult)
                    self.link(dve, last)
                    if gamma is not None:
                        self.link(dve, nc.vector.tensor_tensor(rows_view(to), rows_view(to), row(gamma), ALU.mult))
                        self.link(dve, nc.vector.tensor_tensor(rows_view(to), rows_view(to), row(beta), ALU.add))

                @block.scalar
                def _(sc):
                    sc.wait_ge(self.dve_done.sem, self.dve_done.at)
                    nc.scalar.activation(root, var, ACT.Sqrt).then_inc(self.act_done.sem, 1)
                    self.act_done.up()

    def dve_steps(self, program):
        with self.nc.Block() as block:
            @block.vector
            def _(dve):
                program(lambda ins: self.link(dve, ins))

    def constants(self):
        nc = self.nc
        self.ident = self.sb("ident", [P, P])
        self.before = self.sb("before", [P, P])
        self.iota_w = self.sb("iota_w", [P, 2 * P])
        self.iota_p = self.sb("iota_p", [P, 2])
        self.iota_h = self.sb("iota_h", [P, NT], BF16)
        self.zeros = self.sb("zeros", [P, BANK])
        with self.scope():
            self._fill_constants(self.sb("iw", [P, 2 * P], I32), self.sb("ip", [P, 2], I32))

    def _fill_constants(self, iw, ip):
        nc = self.nc
        made = self.pool_done.at
        with nc.Block() as block:
            @block.gpsimd
            def _(pool):
                nc.gpsimd.memset(self.ident[:], 0.0).then_inc(self.pool_done.sem, 1)
                nc.gpsimd.memset(self.before[:], 0.0).then_inc(self.pool_done.sem, 1)
                pool.wait_ge(self.pool_done.sem, made + 2)
                nc.gpsimd.affine_select(out=self.ident[:], in_=self.ident[:], compare_op=ALU.not_equal, fill=1.0, base=0,
                                        pattern=[[-1, P]], channel_multiplier=1).then_inc(self.pool_done.sem, 1)
                nc.gpsimd.affine_select(out=self.before[:], in_=self.before[:], compare_op=ALU.is_ge, fill=1.0, base=0,
                                        pattern=[[-1, P]], channel_multiplier=1).then_inc(self.pool_done.sem, 1)
                nc.gpsimd.iota(iw[:], pattern=[[1, 2 * P]], base=0, channel_multiplier=0).then_inc(self.pool_done.sem, 1)
                nc.gpsimd.iota(ip[:], pattern=[[P, 2]], base=0, channel_multiplier=1).then_inc(self.pool_done.sem, 1)
                self.pool_done.up(6)
                pool.wait_ge(self.pool_done.sem, self.pool_done.at)

            @block.vector
            def _(dve):
                self.link(dve, nc.vector.memset(self.zeros[:], 0.0))
                dve.wait_ge(self.pool_done.sem, self.pool_done.at)
                self.link(dve, nc.vector.tensor_copy(self.iota_w[:], iw[:]))
                self.link(dve, nc.vector.tensor_copy(self.iota_p[:], ip[:]))
                self.link(dve, nc.vector.tensor_copy(self.iota_h[:], iw[:, 0:NT]))

    def c_to_a(self, pairs):
        nc = self.nc
        ps = self.ps[:].rearrange("p (h c e) -> p h c e", h=4, c=8)
        turned = []
        drained = self.dve_done.at
        with nc.Block() as block:
            @block.tensor
            def _(pe):
                for n, (to, of) in enumerate(pairs):
                    if n >= 4:
                        pe.wait_ge(self.dve_done.sem, drained + n - 3)
                    for c in range(CH):
                        last = nc.tensor.transpose(ps[:, n % 4, c, 0:CT], of[:, c, :], self.ident[0:CT, 0:CT])
                    last.then_inc(self.pe_done.sem, 1)
                    turned.append(self.pe_done.up())

            @block.vector
            def _(dve):
                for n, (to, of) in enumerate(pairs):
                    dve.wait_ge(self.pe_done.sem, turned[n])
                    nc.vector.tensor_copy(to.rearrange("p (c t) -> p c t", c=CH), ps[:, n % 4, 0:CH, 0:CT]).then_inc(self.dve_done.sem, 1)
                    self.dve_done.up()
                dve.wait_ge(self.dve_done.sem, self.dve_done.at)

    def a_to_c(self, pairs):
        nc = self.nc
        ps = self.ps[:].rearrange("p (h c e) -> p h c e", h=4, c=8)
        turned = []
        drained = self.dve_done.at
        with nc.Block() as block:
            @block.tensor
            def _(pe):
                for n, (to, of) in enumerate(pairs):
                    if n >= 4:
                        pe.wait_ge(self.dve_done.sem, drained + n - 3)
                    for c in range(CH):
                        last = nc.tensor.transpose(ps[0:CT, n % 4, c, :], of[:, c * CT:(c + 1) * CT], self.ident[:])
                    last.then_inc(self.pe_done.sem, 1)
                    turned.append(self.pe_done.up())

            @block.vector
            def _(dve):
                for n, (to, of) in enumerate(pairs):
                    dve.wait_ge(self.pe_done.sem, turned[n])
                    nc.vector.tensor_copy(to, ps[0:CT, n % 4, 0:CH, :]).then_inc(self.dve_done.sem, 1)
                    self.dve_done.up()
                dve.wait_ge(self.dve_done.sem, self.dve_done.at)

    def edge_lists(self):
        nc, a = self.nc, self.a
        self.dstx = self.dram("dstx", [EP + 2], I32)
        self.srcx = self.dram("srcx", [EP], I32)
        self.wx = self.dram("wx", [EP])
        self.w1x = self.dram("w1x", [EP])
        self.agg_max = self.dram("agg_max", [NP, D])
        self.agg = self.dram("agg", [NP, D])
        self.agg3 = self.dram("agg3", [NP, D + HEADS])
        pad = EP - E
        ends = self.sb("ends", [1, pad + 2], I32)
        zi = self.sb("zi", [1, pad], I32)
        low = self.sb("low", [P, D])
        none3 = self.sb("none3", [P, D + HEADS])

        @self.dve_steps
        def _(link):
            link(nc.vector.memset(ends[0:1, 0:1], -1))
            link(nc.vector.memset(ends[0:1, 1:], PADDST))
            link(nc.vector.memset(ends[0:1, pad + 1:], PADDST + 1))
            link(nc.vector.memset(zi[:], 0))
            link(nc.vector.memset(low[:], LOWEST))
            link(nc.vector.memset(none3[:, 0:D], 0.0))
            link(nc.vector.memset(none3[:, D:], 1.0))
        row = lambda v: v.rearrange("(a n) -> a n", a=1)
        wide = lambda v: v.rearrange("(a n) -> a n", a=16)
        pairs = [(wide(self.dstx[1:E + 1]), wide(a["dst"])), (wide(self.srcx[0:E]), wide(a["src"])),
                 (wide(self.wx[0:E]), wide(a["edge_weight"])),
                 (wide(self.w1x[0:E]), wide(a["edge_weight1"].rearrange("n o -> (n o)"))),
                 (row(self.dstx[0:1]), ends[0:1, 0:1]), (row(self.dstx[E + 1:]), ends[0:1, 1:]),
                 (row(self.srcx[E:]), zi[:]),
                 (row(self.wx[E:]), self.zeros[0:1, 0:pad]), (row(self.w1x[E:]), self.zeros[0:1, 0:pad])]
        tiles = lambda v: v.rearrange("(i p) f -> p i f", p=P)
        pairs += [(tiles(self.agg_max), low[:].unsqueeze(1).to_broadcast([P, NT, D])),
                  (tiles(self.agg), self.zeros[:, 0:D].unsqueeze(1).to_broadcast([P, NT, D])),
                  (tiles(self.agg3), none3[:].unsqueeze(1).to_broadcast([P, NT, D + HEADS]))]
        self.load(pairs)

    def edge_structure(self):
        nc = self.nc
        by_b = lambda v: v.rearrange("(p j) -> p j", p=P)
        by_c = lambda v: v.rearrange("(c t e) -> t c e", c=CH, t=CT)
        self.rel_a, self.end_a, self.w_a = (self.sb(n, [P, TILES]) for n in ("rel_a", "end_a", "w_a"))
        self.ends3 = self.sb("ends3", [P, PARTS, 2, TILES], BF16)
        self.idx_a = self.sb("idx_a", [P, TILES], I32)
        self.hi16_a = self.sb("hi16_a", [P, TILES], BF16)
        self.window = self.sb("window", [1, TILES], I32)
        self.w1_b = self.sb("w1_b", [P, J])
        self.b = {n: self.sb("b_" + n, [P, J]) for n in
                  ("go_f", "go_g", "neg_f", "neg_g", "open_f", "open_g", "cut_f", "cut_g")}
        self.cut_row = self.sb("cut_row", [HEADS, 4, P])
        with self.scope():
            self._edge_structure(by_b, by_c)

    def _edge_structure(self, by_b, by_c):
        nc = self.nc
        cur, prev, nxt = (self.sb(n, [P, J], I32) for n in ("cur", "prev", "nxt"))
        self.load([(cur[:], by_b(self.dstx[1:EP + 1])), (prev[:], by_b(self.dstx[0:EP])), (nxt[:], by_b(self.dstx[2:EP + 2])),
                   (self.w1_b[:], by_b(self.w1x))])
        b = dict(self.b, start=self.sb("start", [P, J]), end=self.sb("end", [P, J]))
        ones, zeros = self.sb("ones_j", [P, J]), self.sb("zeros_j", [P, J])
        self.cut_col = self.sb("cut_col", [P, 2, HEADS])
        rank = self.sb("rank", [P, J])
        off = self.sb("off", [P, 1])
        neg16 = self.sb("neg16", [P, J], BF16)
        rev = lambda t: t[:, ::-1]

        @self.dve_steps
        def _(link):
            link(nc.vector.memset(ones[:], 1.0))
            link(nc.vector.memset(zeros[:], 0.0))
            link(nc.vector.tensor_tensor(b["start"][:], cur[:], prev[:], ALU.not_equal))
            link(nc.vector.tensor_tensor(b["end"][:], cur[:], nxt[:], ALU.not_equal))
            link(nc.vector.tensor_scalar(b["go_f"][:], b["start"][:], -1.0, 1.0, ALU.mult, ALU.add))
            link(nc.vector.tensor_scalar(b["go_g"][:], b["end"][:], -1.0, 1.0, ALU.mult, ALU.add))
            link(nc.vector.tensor_scalar(b["neg_f"][:], b["start"][:], -BIG, None, ALU.mult))
            link(nc.vector.tensor_scalar(b["neg_g"][:], b["end"][:], -BIG, None, ALU.mult))
            link(nc.vector.tensor_copy(neg16[:], b["neg_f"][:]))
            link(nc.vector.tensor_tensor_scan(out=b["open_f"][:], data0=b["go_f"][:], data1=zeros[:], initial=1.0,
                                              op0=ALU.mult, op1=ALU.add))
            link(nc.vector.tensor_tensor_scan(out=rev(b["open_g"]), data0=rev(b["go_g"]), data1=zeros[:], initial=1.0,
                                              op0=ALU.mult, op1=ALU.add))
            link(nc.vector.tensor_scalar(b["cut_f"][:], b["open_f"][:], BIG, -BIG, ALU.mult, ALU.add))
            link(nc.vector.tensor_scalar(b["cut_g"][:], b["open_g"][:], BIG, -BIG, ALU.mult, ALU.add))
            link(nc.vector.tensor_tensor_scan(out=rank[:], data0=ones[:], data1=b["start"][:], initial=0.0,
                                              op0=ALU.mult, op1=ALU.add))
            link(nc.vector.tensor_copy(self.cut_col[:, 0, :], b["open_f"][:, J - 1:J].to_broadcast([P, HEADS])))
            link(nc.vector.tensor_copy(self.cut_col[:, 1, :], b["open_g"][:, 0:1].to_broadcast([P, HEADS])))
        ps = self.ps
        summed = self.pe_done.at + 1
        with nc.Block() as block:
            @block.tensor
            def _(pe):
                nc.tensor.matmul(ps[:, 0:1], self.before[:], rank[:, J - 1:J], start=True, stop=True)
                nc.tensor.matmul(ps[0:HEADS, BANK:BANK + P], self.cut_col[:, 0, :], self.ident[:], start=True, stop=True)
                nc.tensor.matmul(ps[0:HEADS, 2 * BANK:2 * BANK + P], self.cut_col[:, 1, :], self.ident[:],
                                 start=True, stop=True).then_inc(self.pe_done.sem, 1)
                self.pe_done.up()

            @block.vector
            def _(dve):
                dve.wait_ge(self.pe_done.sem, summed)
                self.link(dve, nc.vector.tensor_copy(off[:], ps[:, 0:1]))
                self.link(dve, nc.vector.tensor_scalar(rank[:], rank[:], off[:, 0:1], -1.0, ALU.add, ALU.add))
                for n in range(2):
                    row = ps[0:HEADS, (n + 1) * BANK:(n + 1) * BANK + P]
                    self.link(dve, nc.vector.tensor_copy(self.cut_row[:, n, :], row))
                    self.link(dve, nc.vector.tensor_scalar(self.cut_row[:, 2 + n, :], row, BIG, -BIG, ALU.mult, ALU.add))
        rank_d, end_d = self.dram("rank_d", [EP]), self.dram("end_d", [EP])
        self.neg_d = self.dram("neg_d", [EP], BF16)
        self.load([(by_b(rank_d), rank[:]), (by_b(end_d), b["end"][:]), (by_b(self.neg_d), neg16[:])])
        rank_c, end_c, w_c = (self.sb(n, [CT, CH, P]) for n in ("rank_c", "end_c", "w_c"))
        src_c, dst_c = (self.sb(n, [CT, CH, P], I32) for n in ("src_c", "dst_c"))
        self.load([(rank_c[:], by_c(rank_d)), (end_c[:], by_c(end_d)), (w_c[:], by_c(self.wx)),
                   (src_c[:], by_c(self.srcx)), (dst_c[:], by_c(self.dstx[1:EP + 1]))])
        base_i = self.sb("base_i", [CT, CH], I32)
        window = self.sb("window_c", [CT, CH], I32)
        base_f = self.sb("base_f", [CT, CH])
        lo_i, hi_i = (self.sb(n, [CT, CH, P], I32) for n in ("lo_i", "hi_i"))
        src_f, hi_f, dst_f, rel_f = (self.sb(n, [CT, CH, P]) for n in ("src_f", "hi_f", "dst_f", "rel_f"))
        lo16, rel16 = (self.sb(n, [CT, CH, P], BF16) for n in ("lo16", "rel16"))
        v = nc.vector

        @self.dve_steps
        def _(link):
            link(v.tensor_copy(base_i[:], rank_c[:, :, 0]))
            link(v.tensor_scalar(base_i[:], base_i[:], 7, 7, ALU.logical_shift_right, ALU.logical_shift_left))
            link(v.tensor_scalar(base_f[:], base_i[:], float(LASTB), None, ALU.min))
            link(v.tensor_scalar(window[:], base_f[:], 1 / P, None, ALU.mult))
            link(v.tensor_tensor(rel_f[:], rank_c[:], base_f[:].unsqueeze(2).to_broadcast([CT, CH, P]), ALU.subtract))
            link(v.tensor_copy(rel16[:], rel_f[:]))
            link(v.tensor_scalar(lo_i[:], src_c[:], P - 1, None, ALU.bitwise_and))
            link(v.tensor_scalar(hi_i[:], src_c[:], 7, None, ALU.logical_shift_right))
            link(v.tensor_copy(lo16[:], lo_i[:]))
            link(v.tensor_copy(hi_f[:], hi_i[:]))
            link(v.tensor_copy(src_f[:], src_c[:]))
            link(v.tensor_scalar(dst_f[:], dst_c[:], 1.0, None, ALU.add))
        window_d = self.dram("window_d", [1, TILES], I32)
        self.lo_d, self.rel_d = self.dram("lo_d", [EP], BF16), self.dram("rel_d", [EP], BF16)
        with nc.allow_non_contiguous_dma(reason="784 window bases, once"):
            self.load([(window_d.rearrange("o (c t) -> t c o", c=CH), window[:].unsqueeze(2)),
                       (by_c(self.lo_d), lo16[:]), (by_c(self.rel_d), rel16[:])])
        self.load([(self.window[:], window_d)])
        self.src_a, self.hi_a = (self.sb(n, [P, TILES]) for n in ("src_a", "hi_a"))
        ends, rest = (self.sb(n, [P, 2, TILES]) for n in ("ends", "rest"))
        number = self.sb("number", [P, TILES], I32)
        self.c_to_a([(self.rel_a[:], rel_f), (self.end_a[:], end_c), (self.w_a[:], w_c), (ends[:, 0, :], dst_f),
                     (self.src_a[:], src_f), (self.hi_a[:], hi_f)])

        with nc.Block() as block:
            @block.gpsimd
            def _(pool):
                nc.gpsimd.iota(number[:], pattern=[[P, TILES]], base=0, channel_multiplier=1).then_inc(self.pool_done.sem, 1)
                self.pool_done.up()
                pool.wait_ge(self.pool_done.sem, self.pool_done.at)

        @self.dve_steps
        def _(link):
            link(v.tensor_copy(self.idx_a[:], self.src_a[:]))
            link(v.tensor_copy(self.hi16_a[:], self.hi_a[:]))
            link(v.tensor_copy(ends[:, 1, :], number[:]))
            self.split(link, ends[:], [self.ends3[:, n] for n in range(PARTS)], rest[:])

    def _gathers(self, block, table, wait_free, tile0=0, iters=ITERS, shares=None):
        nc = self.nc
        staged0 = self.idx_staged.at

        @block.gpsimd
        def _(pool):
            pool.wait_ge(self.loaded.sem, self.loaded.at)
            def gather(i, g):
                pool.wait_ge(self.idx_staged.sem, staged0 + 1 + i * NG + g)
                pool.sem_inc(self.group_begun.sem, 1)
                for k in range(G):
                    t = g * G + k
                    nc.gpsimd.indirect_dma_start(
                        out=self.rows[:, t, :], out_offset=None, in_=table,
                        in_offset=bass.IndirectOffsetOnAxis(ap=self.idx_now[:, t:t + 1], axis=0),
                    ).then_inc(self.gathered[g].sem, 16)

            for g in range(NG):
                gather(0, g)
            with pool.Fori(1, iters) as i:
                for g in range(NG):
                    wait_free(pool, i, g)
                    gather(i, g)
            if shares:
                by_edge, by_rank = shares
                for i in range(NT):
                    nc.gpsimd.indirect_dma_start(
                        out=by_rank[:, i, :], out_offset=None, in_=by_edge,
                        in_offset=bass.IndirectOffsetOnAxis(ap=self.last_i[:, i:i + 1], axis=0)).then_inc(self.stored.sem, 16)
                    self.stored.up(16)
                pool.wait_ge(self.stored.sem, self.stored.at)
        self.idx_staged.up(NG * iters)

    def _stage(self, i, g, tile0=0):
        self.nc.scalar.copy(self.idx_now[:, g * G:(g + 1) * G],
                            self.idx_a[:, bass.ds(tile0 + i * U + g * G, G)]).then_inc(self.idx_staged.sem, 1)

    def _gather_ahead(self, block, table, groups):
        iters = groups // NG
        gathered0, kept0 = self.gathered[0].at, self.rows_kept[0].at
        self._gathers(block, table, lambda pool, i, g: pool.wait_ge(self.rows_kept[g].sem, kept0 + 16 * i), iters=iters)

        @block.scalar
        def _(sc):
            def keep(i, g):
                sc.wait_ge(self.gathered[g].sem, gathered0 + (i + 1) * 16 * G)
                sc.dma_start(self.ahead_group(i * NG + g), self.rows[:, g * G:(g + 1) * G, :].rearrange(
                    "p t f -> p (t f)")).then_inc(self.rows_kept[g].sem, 16)

            for g in range(NG):
                self._stage(0, g)
            with sc.Fori(0, iters - 1) as i:
                for g in range(NG):
                    keep(i, g)
                    self._stage(i + 1, g)
            for g in range(NG):
                keep(iters - 1, g)
            for g in range(NG):
                sc.wait_ge(self.rows_kept[g].sem, kept0 + 16 * iters)
        for g in range(NG):
            self.rows_kept[g].up(16 * iters)
            self.gathered[g].up(16 * G * iters)

    def ahead_group(self, n):
        return self.ahead[bass.ds(n, 1)].rearrange("a p f -> p (a f)")

    def split(self, link, of, parts, rest):
        v = self.nc.vector
        link(v.tensor_copy(parts[0], of))
        link(v.tensor_tensor(rest, of, parts[0], ALU.subtract))
        link(v.tensor_copy(parts[1], rest))
        link(v.tensor_tensor(rest, rest, parts[1], ALU.subtract))
        link(v.tensor_copy(parts[2], rest))

    def clear_accumulator(self):
        for b in range(8):
            self.nc.tensor.matmul(self.ps[:, b * BANK:(b + 1) * BANK], self.zeros[:, 0:P], self.zeros[:], start=True, stop=True)

    def _accumulate(self, pe, tile0, buffer, regs, rows, extra=None, tiles=range(G)):
        nc, ps = self.nc, self.ps
        for k in tiles:
            w = pe.snap(regs[k], min_val=0, max_val=LASTB // P)
            for half in range(2):
                ind = self.ind[:, buffer, k, half * P:(half + 1) * P]
                last = nc.tensor.matmul(ps[:, bass.ds(w * P + half * P, D)], ind, rows[k], start=False, stop=True, skip_group_check=True)
            if extra is not None:
                values, width = extra
                for half in range(2):
                    ind = self.ind[:, buffer, k, half * P:(half + 1) * P].bitcast(BF16)[:, 1::2]
                    last = nc.tensor.matmul(ps[:, bass.ds(w * width + (EXTRA + half * width), width)], ind,
                                            values[:, :, bass.ds(tile0 + k, 1)], start=False, stop=True, skip_group_check=True)
        if tiles[-1] == G - 1:
            last.then_inc(self.tiles_summed.sem, 1)

    def _windows(self, pe, tile0, regs):
        pe.load(regs, self.window[0:1, bass.ds(tile0, len(regs))])

    def sum_pass(self, table, alpha, heads=False, ahead=0, shares=None):
        with self.scope():
            self._ring()
            self.ind = self.sb("ind", [P, 2, G, 2 * P])
            self._sum_pass(table, alpha, heads, ahead, shares)

    def _ring(self):
        self.idx_now = self.sb("idx_now", [P, U], I32)
        self.rows = self.sb("rows", [P, U, D])

    def _sum_pass(self, table, alpha, heads, ahead, shares):
        nc = self.nc
        iters = ITERS - ahead // NG
        slots = ahead // iters // 2 * 2
        order = [kind for g in range(NG) for kind in
                 [("ahead", s) for s in range(slots) if s * NG // slots == g] + [("ring", g)]]
        step, late = len(order), ahead - slots * iters
        assert step % 2 == 0 and 0 <= late
        at = {kind: n for n, kind in enumerate(order)}
        summed0, built0, gathered0 = self.tiles_summed.at, self.ind_built.at, self.gathered[0].at
        ahead0 = [arrived.at for arrived in self.ahead_in]
        early = self.sb("early", [P, max(slots, 1), G, D])
        self.tiles_summed.up(step)

        def rows_in(engine, kind, n, i):
            if kind == "ring":
                engine.wait_ge(self.gathered[n].sem, gathered0 + (i + 1) * 16 * G)
            else:
                engine.wait_ge(self.ahead_in[n].sem, ahead0[n] + (i + 1) * 16)

        def place(kind, n, k=None):
            rows = self.rows[:, n * G:(n + 1) * G, :] if kind == "ring" else early[:, n]
            return rows if k is None else rows[:, k, :]

        def groups(i):
            for kind, n in order:
                yield (i * step + at[kind, n], kind, n, (ahead * G + i * U + n * G) if kind == "ring" else (i * slots + n) * G, i)

        def late_groups():
            for m in range(late):
                yield iters * step + m, "ahead", m % slots, (iters * slots + m) * G, iters + m // slots

        with nc.Block() as block:
            self._gathers(block, table, lambda pool, i, g: pool.wait_ge(self.tiles_summed.sem, summed0 + i * step + at["ring", g] + 1),
                          ahead * G, iters, shares)

            @block.scalar
            def _(sc):
                with sc.Fori(0, iters) as i:
                    for g in range(NG):
                        sc.wait_ge(self.gathered[g].sem, gathered0 + i * 16 * G)
                        self._stage(i, g, ahead * G)

            if ahead:
                @block.sync
                def _(sp):
                    with sp.Fori(0, iters) as i:
                        for s in range(slots):
                            sp.wait_ge(self.tiles_summed.sem, summed0 + i * step + at["ahead", s] + 1)
                            sp.dma_start(early[:, s].rearrange("p t f -> p (t f)"), self.ahead_group(i * slots + s)).then_inc(self.ahead_in[s].sem, 16)
                    for m in range(late):
                        before = iters * step + at["ahead", m] if m < slots else (iters + 1) * step + m - slots
                        sp.wait_ge(self.tiles_summed.sem, summed0 + before + 1)
                        sp.dma_start(early[:, m % slots].rearrange("p t f -> p (t f)"),
                                     self.ahead_group(iters * slots + m)).then_inc(self.ahead_in[m % slots].sem, 16)

            @block.vector
            def _(dve):
                dve.sem_inc(self.tiles_summed.sem, step)

                def build(number, kind, n, tile0, i, buffer):
                    dve.wait_ge(self.tiles_summed.sem, summed0 + step - 1 + number)
                    for k in range(G):
                        col = bass.ds(tile0 + k, 1)
                        ind = self.ind[:, buffer, k, :]
                        if heads:
                            last = nc.vector.tensor_scalar(ind, self.iota_w[:], self.rel_a[:, col], None, ALU.is_equal)
                        else:
                            last = nc.vector.tensor_scalar(ind, self.iota_w[:], self.rel_a[:, col], alpha[:, 0, col],
                                                           ALU.is_equal, ALU.mult)
                    if heads:
                        rows_in(dve, kind, n, i)
                        v = place(kind, n).rearrange("p t (h c) -> p t h c", h=HEADS)
                        al = alpha[:, :, bass.ds(tile0, G)].rearrange("p h t -> p t h").unsqueeze(3)
                        last = nc.vector.tensor_tensor(v, v, al.to_broadcast([P, G, HEADS, HD]), ALU.mult)
                    last.then_inc(self.ind_built.sem, 1)

                with dve.Fori(0, iters) as i:
                    for m, group in enumerate(groups(i)):
                        build(*group, m % 2)
                for m, group in enumerate(late_groups()):
                    build(*group, m % 2)

            @block.tensor
            def _(pe):
                with ExitStack() as st:
                    regs = [st.enter_context(nc.tensor.register(f"window{n}_{self.names}")) for n in range(G)]

                    def total(number, kind, n, tile0, i, buffer):
                        self._windows(pe, tile0, regs)
                        pe.wait_ge(self.ind_built.sem, built0 + 1 + number)
                        rows_in(pe, kind, n, i)
                        self._accumulate(pe, tile0, buffer, regs, [place(kind, n, k) for k in range(G)])

                    self.clear_accumulator()
                    with pe.Fori(0, iters) as i:
                        for m, group in enumerate(groups(i)):
                            total(*group, m % 2)
                    for m, group in enumerate(late_groups()):
                        total(*group, m % 2)
        self.tiles_summed.up(step * iters + late)
        self.ind_built.up(step * iters + late)
        for g in range(NG):
            self.gathered[g].up(16 * G * iters)
        for s in range(slots):
            self.ahead_in[s].up(16 * (iters + len(range(s, late, slots))))

    def max_pass(self, table):
        with self.scope():
            self._ring()
            self.ind = self.sb("ind", [P, 2, G, 2 * P])
            self.scan = self.sb("scan", [P, 2, G * P])
            self.back = self.sb("back", [P, 2, G, D])
            self.mask = self.sb("mask", [P, NG, G * P], BF16)
            self._max_pass(table)

    def _max_pass(self, table):
        nc, ps = self.nc, self.ps
        scan, back = self.scan, self.back

        @self.dve_steps
        def _(link):
            link(nc.vector.memset(scan[:], -BIG))
        extra = (self.ends3[:].rearrange("p s k t -> p (s k) t"), 2 * PARTS)
        summed0, built0, gathered0, mask0 = self.tiles_summed.at, self.ind_built.at, self.gathered[0].at, self.mask_in[0].at
        turned0, scanned0, out0, drained0 = self.rows_turned.at, self.scanned.at, self.scan_turned.at, self.turned_out.at
        with nc.Block() as block:
            self._gathers(block, table, lambda pool, i, g: pool.wait_ge(self.rows_turned.sem, turned0 + i * NG + g + 1))

            @block.sync
            def _(sp):
                with sp.Fori(0, ITERS) as i:
                    for g in range(NG):
                        sp.wait_ge(self.scanned.sem, scanned0 + i * NG + g + 1)
                        sp.dma_start(self.mask[:, g, :], self.neg_d.rearrange("(a n) -> a n", a=1)[
                            :, bass.ds(i * (U * P) + g * G * P, G * P)].to_broadcast([P, G * P])).then_inc(self.mask_in[g].sem, 16)

            @block.vector
            def _(dve):
                dve.sem_inc(self.rows_turned.sem, NG)
                dve.sem_inc(self.scanned.sem, NG)
                dve.sem_inc(self.turned_out.sem, 1)
                dve.sem_inc(self.tiles_summed.sem, 2)
                with dve.Fori(0, ITERS) as i:
                    for g in range(NG):
                        dve.wait_ge(self.tiles_summed.sem, summed0 + 1 + i * NG + g)
                        for k in range(G):
                            col = bass.ds(i * U + g * G + k, 1)
                            last = nc.vector.tensor_scalar(self.ind[:, g % 2, k, :], self.iota_w[:], self.rel_a[:, col],
                                                           self.end_a[:, col], ALU.is_equal, ALU.mult)
                        last.then_inc(self.ind_built.sem, 1)
                        dve.wait_ge(self.rows_turned.sem, turned0 + NG + 1 + i * NG + g)
                        dve.wait_ge(self.mask_in[g].sem, mask0 + (i + 1) * 16)
                        dve.wait_ge(self.scanned.sem, scanned0 + NG + i * NG + g)
                        nc.vector.tensor_tensor_scan(
                            out=scan[:, g % 2, :], data0=self.mask[:, g, :], data1=ps[:, TURN:TURN + G * P],
                            initial=scan[:, (g + 1) % 2, G * P - 1:G * P], op0=ALU.add, op1=ALU.max).then_inc(self.scanned.sem, 1)

            @block.scalar
            def _(sc):
                for g in range(NG):
                    self._stage(0, g)

                def drain(i, g, stage):
                    if stage:
                        sc.wait_ge(self.gathered[g].sem, gathered0 + (i + 1) * 16 * G)
                        self._stage(i + 1, g)
                    sc.wait_ge(self.scan_turned.sem, out0 + 1 + i * NG + g)
                    sc.wait_ge(self.tiles_summed.sem, summed0 + 1 + i * NG + g)
                    nc.scalar.copy(back[:, g % 2], ps[:, TURN:TURN + G * P].rearrange(
                        "p (t f) -> p t f", t=G)).then_inc(self.turned_out.sem, 1)

                with sc.Fori(0, ITERS - 1) as i:
                    for g in range(NG):
                        drain(i, g, True)
                for g in range(NG):
                    drain(ITERS - 1, g, False)

            @block.tensor
            def _(pe):
                with ExitStack() as st:
                    regs = [st.enter_context(nc.tensor.register(f"window{n}_{self.names}")) for n in range(G)]

                    def turn_in(i, g):
                        pe.wait_ge(self.gathered[g].sem, gathered0 + (i + 1) * 16 * G)
                        pe.wait_ge(self.turned_out.sem, drained0 + 1 + i * NG + g)
                        for k in range(G):
                            last = nc.tensor.transpose(ps[:, TURN + k * P:TURN + (k + 1) * P], self.rows[:, g * G + k, :], self.ident[:])
                        last.then_inc(self.rows_turned.sem, 1)

                    def turn_back(i, g):
                        pe.wait_ge(self.scanned.sem, scanned0 + NG + 1 + i * NG + g)
                        for k in range(G):
                            last = nc.tensor.transpose(ps[:, TURN + k * P:TURN + (k + 1) * P], scan[:, g % 2, k * P:(k + 1) * P], self.ident[:])
                        last.then_inc(self.scan_turned.sem, 1)

                    def sum_half(i, g, half):
                        if half == 0:
                            self._windows(pe, i * U + g * G, regs)
                            pe.wait_ge(self.turned_out.sem, drained0 + 2 + i * NG + g)
                            pe.wait_ge(self.ind_built.sem, built0 + 1 + i * NG + g)
                        self._accumulate(pe, i * U + g * G, g % 2, regs, [back[:, g % 2, k, :] for k in range(G)], extra,
                                         range(2 * half, 2 * half + 2))

                    def groups(i, first):
                        for g in range(NG):
                            before = None if first and g == 0 else (i, g - 1) if g else (i - 1, NG - 1)
                            turn_in(i, g)
                            if before:
                                sum_half(*before, 0)
                            turn_back(i, g)
                            if before:
                                sum_half(*before, 1)

                    self.clear_accumulator()
                    groups(0, True)
                    with pe.Fori(1, ITERS) as i:
                        groups(i, False)
                    sum_half(ITERS - 1, NG - 1, 0)
                    sum_half(ITERS - 1, NG - 1, 1)
        q = NG * ITERS
        self.rows_turned.up(NG + q)
        self.scanned.up(NG + q)
        self.turned_out.up(1 + q)
        self.scan_turned.up(q)
        self.tiles_summed.up(2 + q)
        self.ind_built.up(q)
        for g in range(NG):
            self.gathered[g].up(16 * G * ITERS)
            self.mask_in[g].up(16 * ITERS)

    def rank_nodes(self):
        nc, ps = self.nc, self.ps
        node = self.sb("node", [P, NT, 2])
        none = self.sb("none", [P, NT])
        v = nc.vector

        @self.dve_steps
        def _(link):
            link(v.tensor_reduce(node[:], ps[:, EXTRA:EXTRA + NT * PARTS * 2].rearrange("p (i s k) -> p i k s", s=PARTS, k=2),
                                 AX_X, ALU.add))
            link(v.tensor_copy(self.last_i[:], node[:, :, 1]))
            link(v.tensor_scalar(none[:], node[:, :, 0], 0.5, float(FARIDX), ALU.is_lt, ALU.mult))
            link(v.tensor_scalar(node[:, :, 0], node[:, :, 0], -1.0, None, ALU.add))
            link(v.tensor_tensor(self.node_i[:], node[:, :, 0], none[:], ALU.add))

    def to_nodes(self, dram, to, beside=None):
        with self.scope():
            self._to_nodes(dram, self.sb("by_rank", [P, NT, dram.shape[1]]), beside)
        self.load([(to, dram.rearrange("(i p) f -> p i f", p=P))])

    def _to_nodes(self, dram, out, beside):
        nc, ps = self.nc, self.ps
        first = self.dve_done.at + (beside is not None)
        with nc.Block() as block:
            @block.vector
            def _(dve):
                if beside is not None:
                    nc.vector.tensor_copy(out[:, :, D:], beside).then_inc(self.dve_done.sem, 1)
                for b in range(NBANK):
                    lo, hi = bank(b)
                    nc.vector.tensor_copy(out[:, lo // D:hi // D, 0:D], ps[:, lo:hi].rearrange(
                        "p (i f) -> p i f", f=D)).then_inc(self.dve_done.sem, 1)

            @block.gpsimd
            def _(pool):
                for i in range(NT):
                    if i * D % BANK == 0:
                        pool.wait_ge(self.dve_done.sem, first + i * D // BANK + 1)
                        pool.sem_inc(self.group_begun.sem, 1)
                    nc.gpsimd.indirect_dma_start(
                        out=dram, out_offset=bass.IndirectOffsetOnAxis(ap=self.node_i[:, i:i + 1], axis=0),
                        in_=out[:, i, :], in_offset=None, bounds_check=NP - 1, oob_is_err=False,
                    ).then_inc(self.stored.sem, 16)
                    self.stored.up(16)
                pool.wait_ge(self.stored.sem, self.stored.at)
        self.dve_done.up(NBANK + (beside is not None))

    def edge_logits(self, u, ku, kv, table, ahead):
        with self.scope():
            sb = self.sb
            self._ring()
            self.lo_b, self.rel_b = sb("lo_b", [P, 2, H8 * P], BF16), sb("rel_b", [P, 2, H8 * P], BF16)
            self.lo_hot, self.rel_hot = sb("lo_hot", [P, 2, H8 * P], BF16), sb("rel_hot", [P, 2, 2, H8 * P], BF16)
            self.hi_mask = sb("hi_mask", [P, 2, H8, NT], BF16)
            self.prod = sb("prod", [P, 2, H8 * ku * NT])
            self.us, self.vs = sb("us", [P, 2, H8, HEADS]), sb("vs", [P, 2, H8, 2 * HEADS])
            self._edge_logits(u, ku, kv, table, ahead)

    def _edge_logits(self, u, ku, kv, table, ahead):
        nc, ps = self.nc, self.ps
        v = nc.vector
        vr = self.v_rank[:, :, 0:kv]
        u3 = self.u3[:, :, 0:ku, :]
        v3 = self.v3[:, 0:NT * 3 * kv].rearrange("p (i s k) -> p s i k", s=3, k=kv)

        @self.dve_steps
        def _(link):
            self.split(link, u, [u3[:, n] for n in range(3)], self.rest[:, 0:ku * NT].rearrange("p (k i) -> p k i", k=ku))
            self.split(link, vr, [v3[:, n] for n in range(3)], self.rest[:, 0:NT * kv].rearrange("p (i k) -> p i k", k=kv))

        hot0, picked0, read0 = self.hot_built.at, self.picked.at, self.pick_read.at
        lo0, rel0 = self.lo_in[0].at, self.rel_in[0].at
        W = H8 * P
        row = lambda t, i, h: t.rearrange("(a n) -> a n", a=1)[:, bass.ds(i * (U * P) + h * W, W)].to_broadcast([P, W])
        with nc.Block() as block:
            self._gather_ahead(block, table, ahead)

            @block.sync
            def _(sp):
                with sp.Fori(0, ITERS) as i:
                    for h in range(2):
                        sp.wait_ge(self.hot_built.sem, hot0 + 1 + i * 2 + h)
                        sp.dma_start(self.lo_b[:, h, :], row(self.lo_d, i, h)).then_inc(self.lo_in[h].sem, 16)
                        sp.dma_start(self.rel_b[:, h, :], row(self.rel_d, i, h)).then_inc(self.rel_in[h].sem, 16)

            @block.tensor
            def _(pe):
                with ExitStack() as st:
                    regs = [st.enter_context(nc.tensor.register(f"window{n}_{self.names}")) for n in range(H8)]
                    with pe.Fori(0, ITERS) as i:
                        for h in range(2):
                            self._windows(pe, i * U + h * H8, regs)
                            pe.wait_ge(self.hot_built.sem, hot0 + 3 + i * 2 + h)
                            pe.wait_ge(self.pick_read.sem, read0 + 1 + i * 2 + h)
                            for k in range(H8):
                                c = slice(k * P, (k + 1) * P)
                                at = h * 2 * BANK + k * P
                                for n in range(3):
                                    nc.tensor.matmul(ps[:, at:at + ku * NT], self.lo_hot[:, h, c],
                                                     u3[:, n].rearrange("p k i -> p (k i)"), start=n == 0, stop=n == 2)
                                w = pe.snap(regs[k], min_val=0, max_val=LASTB // P)
                                at = (4 + h) * BANK + k * 3 * kv
                                for half in range(2):
                                    last = nc.tensor.matmul(ps[:, at:at + 3 * kv], self.rel_hot[:, h, half, c],
                                                            self.v3[:, bass.ds(w * 3 * kv + half * 3 * kv, 3 * kv)],
                                                            start=half == 0, stop=half == 1)
                            last.then_inc(self.picked.sem, 1)

            @block.vector
            def _(dve):
                dve.sem_inc(self.hot_built.sem, 2)
                dve.sem_inc(self.picked.sem, 2)
                dve.sem_inc(self.pick_read.sem, 2)

                def build(i, h):
                    dve.wait_ge(self.lo_in[h].sem, lo0 + (i + 1) * 16)
                    dve.wait_ge(self.rel_in[h].sem, rel0 + (i + 1) * 16)
                    dve.wait_ge(self.picked.sem, picked0 + 1 + i * 2 + h)
                    v.tensor_scalar(self.lo_hot[:, h, :], self.lo_b[:, h, :], self.iota_p[:, 0:1], None, ALU.is_equal)
                    for half in range(2):
                        v.tensor_scalar(self.rel_hot[:, h, half, :], self.rel_b[:, h, :], self.iota_p[:, half:half + 1], None, ALU.is_equal)
                    v.tensor_tensor(self.hi_mask[:, h], self.iota_h[:].unsqueeze(1).to_broadcast([P, H8, NT]),
                                    self.hi16_a[:, bass.ds(i * U + h * H8, H8)].unsqueeze(2).to_broadcast([P, H8, NT]),
                                    ALU.is_equal).then_inc(self.hot_built.sem, 1)

                def read(i, h):
                    chain0 = self.dve_chain.at
                    dve.wait_ge(self.picked.sem, picked0 + 3 + i * 2 + h)
                    lo = ps[:, h * 2 * BANK:(h + 1) * 2 * BANK].rearrange("p (t c) -> p t c", c=P)[:, :, 0:ku * NT]
                    hi = ps[:, (4 + h) * BANK:(4 + h) * BANK + H8 * 3 * kv].rearrange("p (t s k) -> p t k s", s=3, k=kv)
                    prod = self.prod[:, h, 0:H8 * ku * NT].rearrange("p (t k i) -> p t k i", t=H8, k=ku)
                    us, vs = self.us[:, h, :, 0:ku], self.vs[:, h, :, 0:kv]
                    at = bass.ds(i * U + h * H8, H8)
                    v.tensor_tensor(prod, lo.rearrange("p t (k i) -> p t k i", k=ku),
                                    self.hi_mask[:, h].unsqueeze(2).to_broadcast([P, H8, ku, NT]), ALU.mult).then_inc(self.dve_chain.sem, 1)
                    v.tensor_reduce(vs, hi, AX_X, ALU.add).then_inc(self.dve_chain.sem, 1)
                    dve.wait_ge(self.dve_chain.sem, chain0 + 1 + 3 * (i * 2 + h))
                    v.tensor_reduce(us, prod, AX_X, ALU.add).then_inc(self.dve_chain.sem, 1)
                    dve.wait_ge(self.dve_chain.sem, chain0 + 3 + 3 * (i * 2 + h))
                    last = v.tensor_tensor(self.lg_a[:, 0:ku, at], us.rearrange("p t k -> p k t"),
                                           vs[:, :, 0:ku].rearrange("p t k -> p k t"), ALU.add)
                    if kv > ku:
                        last = v.tensor_copy(self.self_a[:, :, at], vs[:, :, ku:].rearrange("p t k -> p k t"))
                    last.then_inc(self.pick_read.sem, 1)

                build(0, 0)
                with dve.Fori(0, ITERS - 1) as i:
                    build(i, 1)
                    read(i, 0)
                    build(i + 1, 0)
                    read(i, 1)
                build(ITERS - 1, 1)
                read(ITERS - 1, 0)
                read(ITERS - 1, 1)
        q = 2 * ITERS
        self.hot_built.up(2 + q)
        self.picked.up(2 + q)
        self.pick_read.up(2 + q)
        self.dve_chain.up(3 * q)
        for h in range(2):
            self.lo_in[h].up(16 * ITERS)
            self.rel_in[h].up(16 * ITERS)

    def _carries(self, f, g, k, maximum):
        nc, ps = self.nc, self.ps
        turned = self.pe_done.at
        init = -BIG if maximum else 0.0
        op0, op1 = (ALU.add, ALU.max) if maximum else (ALU.mult, ALU.add)
        cut = lambda n: self.cut_row[0:k, (2 if maximum else 0) + n, :]
        c = self.carry_row
        scanned = self.dve_done.at + 1
        with nc.Block() as block:
            @block.tensor
            def _(pe):
                nc.tensor.matmul(ps[0:k, 0:P], f[:, 0:k, J - 1], self.ident[:], start=True, stop=True)
                nc.tensor.matmul(ps[0:k, BANK:BANK + P], g[:, 0:k, 0], self.ident[:], start=True, stop=True).then_inc(self.pe_done.sem, 1)
                pe.wait_ge(self.dve_done.sem, scanned)
                nc.tensor.matmul(ps[:, 2 * BANK:2 * BANK + k], c[0:k, 0, 0:P], self.ident[0:k, 0:k], start=True, stop=True)
                nc.tensor.matmul(ps[:, 3 * BANK:3 * BANK + k], c[0:k, 1, 1:P + 1], self.ident[0:k, 0:k],
                                 start=True, stop=True).then_inc(self.pe_done.sem, 1)
                self.pe_done.up(2)

            @block.vector
            def _(dve):
                self.link(dve, nc.vector.memset(c[:], init))
                dve.wait_ge(self.pe_done.sem, turned + 1)
                nc.vector.tensor_tensor_scan(out=c[0:k, 0, 1:P + 1], data0=cut(0), data1=ps[0:k, 0:P], initial=init, op0=op0, op1=op1)
                nc.vector.tensor_tensor_scan(out=c[0:k, 1, 0:P][:, ::-1], data0=cut(1)[:, ::-1], data1=ps[0:k, BANK:BANK + P][:, ::-1],
                                             initial=init, op0=op0, op1=op1).then_inc(self.dve_done.sem, 1)
                self.dve_done.up()
                dve.wait_ge(self.pe_done.sem, turned + 2)
                self.link(dve, nc.vector.tensor_copy(self.carry[:, 0, 0:k], ps[:, 2 * BANK:2 * BANK + k]))
                self.link(dve, nc.vector.tensor_copy(self.carry[:, 1, 0:k], ps[:, 3 * BANK:3 * BANK + k]))

    def segment_softmax(self, k, slope, dist=None, own=False):
        q = 2 * k if own else k
        qs = [self.lg_a[:, n, :] for n in range(k)] + [self.self_a[:, n, :] for n in range(k) if own]
        lg_d = self.dram(f"lg_d{self.names}", [q, EP])
        al_d = self.dram(f"al_d{self.names}", [k, EP])
        self.names += 1
        by_b = lambda t, n: t[n].rearrange("(p j) -> p j", p=P)
        by_c = lambda t, n: t[n].rearrange("(c t e) -> t c e", c=CH, t=CT)
        with self.scope():
            val_c = self.sb("val_c", [CT, q, CH, P])
            self.a_to_c([(val_c[:, n], qs[n]) for n in range(q)])
            self.load([(by_c(lg_d, n), val_c[:, n]) for n in range(q)])
        with self.scope():
            self.l_b = self.sb("l_b", [P, q, J])
            self.f_b, self.g_b, self.m_b = (self.sb(n, [P, k, J]) for n in ("f_b", "g_b", "m_b"))
            self._softmax_b(k, q, slope, dist, own, lg_d, al_d, by_b)
        with self.scope():
            val_c = self.sb("val_c", [CT, k, CH, P])
            self.load([(val_c[:, n], by_c(al_d, n)) for n in range(k)])
            self.c_to_a([(qs[n], val_c[:, n]) for n in range(k)])

    def _softmax_b(self, k, q, slope, dist, own, lg_d, al_d, by_b):
        nc, v, b = self.nc, self.nc.vector, self.b
        self.load([(self.l_b[:, n, :], by_b(lg_d, n)) for n in range(q)])
        l, f, g, m = self.l_b, self.f_b, self.g_b, self.m_b
        rev = lambda t: t[:, ::-1]

        def scans(link, kinds, op0, op1, init):
            for n in range(k):
                link(v.tensor_tensor_scan(out=f[:, n, :], data0=b[kinds[0]][:], data1=l[:, n, :],
                                          initial=init, op0=op0, op1=op1))
                link(v.tensor_tensor_scan(out=rev(g[:, n, :]), data0=rev(b[kinds[1]]), data1=rev(l[:, n, :]),
                                          initial=init, op0=op0, op1=op1))

        @self.dve_steps
        def _(link):
            if dist is not None:
                link(v.scalar_tensor_tensor(out=l[:, 0, :], in0=self.w1_b[:], scalar=dist, in1=l[:, 0, :],
                                            op0=ALU.mult, op1=ALU.add))
            link(v.scalar_tensor_tensor(out=l[:, 0:q, :], in0=l[:, 0:q, :], scalar=slope, in1=l[:, 0:q, :], op0=ALU.mult, op1=ALU.max))
            scans(link, ("neg_f", "neg_g"), ALU.add, ALU.max, -BIG)

        self._carries(f, g, k, True)

        @self.dve_steps
        def _(link):
            link(v.tensor_tensor(m[:, 0:k, :], f[:, 0:k, :], g[:, 0:k, :], ALU.max))
            for n in range(k):
                for d, cut in enumerate(("cut_f", "cut_g")):
                    link(v.scalar_tensor_tensor(out=m[:, n, :], in0=b[cut][:], scalar=self.carry[:, d, n:n + 1], in1=m[:, n, :],
                                                op0=ALU.add, op1=ALU.max))
            if own:
                link(v.tensor_tensor(m[:, 0:k, :], m[:, 0:k, :], l[:, k:q, :], ALU.max))
                link(v.tensor_tensor(l[:, k:q, :], l[:, k:q, :], m[:, 0:k, :], ALU.subtract))
            link(v.tensor_tensor(l[:, 0:k, :], l[:, 0:k, :], m[:, 0:k, :], ALU.subtract))

        with nc.Block() as block:
            @block.scalar
            def _(sc):
                nc.scalar.activation(l[:, 0:q, :], l[:, 0:q, :], ACT.Exp)

        @self.dve_steps
        def _(link):
            scans(link, ("go_f", "go_g"), ALU.mult, ALU.add, 0.0)

        self._carries(f, g, k, False)

        @self.dve_steps
        def _(link):
            link(v.tensor_tensor(m[:, 0:k, :], f[:, 0:k, :], g[:, 0:k, :], ALU.add))
            link(v.tensor_tensor(m[:, 0:k, :], m[:, 0:k, :], l[:, 0:k, :], ALU.subtract))
            for n in range(k):
                for d, open_ in enumerate(("open_f", "open_g")):
                    link(v.scalar_tensor_tensor(out=m[:, n, :], in0=b[open_][:], scalar=self.carry[:, d, n:n + 1], in1=m[:, n, :],
                                                op0=ALU.mult, op1=ALU.add))
            if own:
                link(v.scalar_tensor_tensor(out=m[:, 0:k, :], in0=l[:, k:q, :], scalar=1e-16, in1=m[:, 0:k, :],
                                            op0=ALU.add, op1=ALU.add))
            link(v.reciprocal(m[:, 0:k, :], m[:, 0:k, :]))
            link(v.tensor_tensor(l[:, 0:k, :], l[:, 0:k, :], m[:, 0:k, :], ALU.mult))
            if own:
                by_edge = f[:].rearrange("p k j -> p (k j)")
                link(v.tensor_tensor(by_edge.rearrange("p (j k) -> p k j", k=k), l[:, k:q, :], m[:, 0:k, :], ALU.mult))

        self.load([(by_b(al_d, n), l[:, n, :]) for n in range(k)]
                  + ([(self.own_d.rearrange("(p j) k -> p (j k)", p=P), f[:].rearrange("p k j -> p (k j)"))] if own else []))

    def store_table(self, rows):
        self.load([(self.table.rearrange("(i p) f -> p i f", p=P), rows[:].rearrange("p (i f) -> p i f", f=D))], wait=False)

    def matrices(self, *names):
        return [self.sb(n, [P, D]) for n in names]

    def nodes(self, *names):
        return [self.sb(n, [P, NP]) for n in names]

    def run(self):
        self.constants()
        self.stat = self.sb("stat", [P, 6, NT])
        self.node_i, self.last_i = (self.sb(n, [P, NT], I32) for n in ("node_i", "last_i"))
        self.y, self.z = self.nodes("y", "z")
        self.ahead = self.dram("ahead", [AHEAD, P, G * D])
        self.table, self.kept = self.dram("table", [NP, D]), self.dram("kept", [NP, D])
        kept = self.kept.rearrange("(i p) f -> p i f", p=P)
        with self.scope():
            self.edge_lists()
        self.edge_structure()
        with self.scope():
            self.x, = self.nodes("x")
            self.layer_of_maxima()
            self.layer_of_sums()

            @self.dve_steps
            def _(link):
                link(self.nc.vector.tensor_copy(self.z[:], self.x[:]))

            self.load([(kept, rows_view(self.x))])
        with self.scope():
            self.attention_buffers()
            self.layer_of_attention()
            self.layer_of_heads()
        view, x = rows_view, self.z
        self.load([(self.out[0:(NT - 1) * P, :].rearrange("(i p) f -> p i f", p=P), view(x)[:, 0:NT - 1, :]),
                   (self.out[(NT - 1) * P:N, :], view(x)[0:TAIL, NT - 1, :])])

    def layer_of_maxima(self):
        a, v, x, y, z, view = self.a, self.nc.vector, self.x, self.y, self.z, rows_view
        with self.scope():
            t1, h_t, t3 = self.nodes("t1", "h_t", "t3")
            w_in, w_up1, w_up2, w_out, g1, be1, g2, be2 = self.matrices("w_in", "w_up1", "w_up2", "w_out", "g1", "be1", "g2", "be2")
            ffn1, ffn2, ffn1_b = self.sb("ffn1", [P, 4 * D]), self.sb("ffn2", [P, 4, D]), self.sb("ffn1_b", [P, 4])
            b_in, b_up, b_out, b_ffn2 = (self.sb(n, [P, 1]) for n in ("b_in", "b_up", "b_out", "b_ffn2"))

            @self.dve_steps
            def _(link):
                link(v.memset(x[:], 0.0))
            with self.nc.allow_non_contiguous_dma(reason="biases of 128 values as columns"):
                self.load([
                    (view(x)[:, 0:NT - 1, :], a["x"][0:(NT - 1) * P, :].rearrange("(i p) f -> p i f", p=P)),
                    (view(x)[0:TAIL, NT - 1, :], a["x"][(NT - 1) * P:N, :]),
                    (w_in[:], a["L0_gnn_W_in_w"]), (w_up1[:], a["L0_gnn_W_upd_w"][0:D, :]), (w_up2[:], a["L0_gnn_W_upd_w"][D:, :]),
                    (w_out[:], a["L0_gnn_W_out_w"]), (g1[:], on_all(a["L0_gnn_ln1_g"])), (be1[:], on_all(a["L0_gnn_ln1_b"])),
                    (g2[:], on_all(a["L0_gnn_ln2_g"])), (be2[:], on_all(a["L0_gnn_ln2_b"])),
                    (ffn1[:], a["L0_gnn_ffn1_w"]), (ffn2[:], a["L0_gnn_ffn2_w"].rearrange("(c k) f -> k c f", k=P)),
                    (b_in[:], column(a["L0_gnn_W_in_b"])), (b_up[:], column(a["L0_gnn_W_upd_b"])),
                    (b_out[:], column(a["L0_gnn_W_out_b"])), (b_ffn2[:], column(a["L0_gnn_ffn2_b"])),
                    (ffn1_b[:], a["L0_gnn_ffn1_b"].rearrange("(c k) -> k c", k=P)),
                ])
            self.turn(t1, x)
            self.linear_t(h_t, [(w_in[:], t1)], b_in[:])
            self.turn(y, h_t)
            self.store_table(y)
            self.max_pass(self.table)
            self.rank_nodes()
            with self.scope():
                agg = self.sb("agg", [P, NT, D])
                self.to_nodes(self.agg_max, agg[:])

                @self.dve_steps
                def _(link):
                    link(v.tensor_tensor(view(y), agg[:], view(y), ALU.subtract))
                    link(v.scalar_tensor_tensor(out=view(y), in0=agg[:], scalar=LOWEST / 3, in1=view(y),
                                                op0=ALU.is_gt, op1=ALU.mult))
            self.turn(t1, y)
            self.linear_t(t3, [(w_up1[:], h_t), (w_up2[:], t1)], b_up[:])
            self.linear_t(h_t, [(w_out[:], t3)], b_out[:])
            self.turn(y, h_t, add=x)
            self.layer_norm(y, y, 1e-5, g1, be1)
            self.turn(t1, y)
            with self.scope():
                hidden = [h_t, t3, z, *self.nodes("t4")]
                for c in range(4):
                    self.linear_t(hidden[c], [(ffn1[:, c * D:(c + 1) * D], t1)], ffn1_b[:, c:c + 1], gelu=True)
                self.linear_t(t1, [(ffn2[:, c, :], hidden[c]) for c in range(4)], b_ffn2[:])
            self.turn(z, t1, add=y)
            self.layer_norm(z, z, 1e-5, g2, be2)

        @self.dve_steps
        def _(link):
            link(v.tensor_tensor(x[:], x[:], z[:], ALU.add))
        self.layer_norm(x, x, 1e-5)

    def layer_of_sums(self):
        nc, a, v, x, y, z, view, st = self.nc, self.a, self.nc.vector, self.x, self.y, self.z, rows_view, self.stat
        self.store_table(x)
        self.sum_pass(self.table, self.w_a[:].unsqueeze(1))
        with self.scope():
            t1, t2, t3 = self.nodes("t1", "t2", "t3")
            w1, w2 = self.matrices("w1", "w2")
            b1, b2, b = (self.sb(n, [P, 1]) for n in ("b1", "b2", "b"))
            agg = self.sb("agg", [P, NT, D])
            with nc.allow_non_contiguous_dma(reason="biases of 128 values as columns"):
                self.load([(w1[:], a["L1_gnn_W1"]), (w2[:], a["L1_gnn_W2"]),
                           (b1[:], a["L1_gnn_b1"].rearrange("o n -> n o")), (b2[:], a["L1_gnn_b2"].rearrange("o n -> n o"))])
            self.to_nodes(self.agg, agg[:])

            @self.dve_steps
            def _(link):
                link(v.tensor_tensor(view(y), agg[:], view(x), ALU.add))
                link(v.tensor_tensor(view(z), agg[:], view(x), ALU.mult))
                link(v.tensor_tensor(b[:], b1[:], b2[:], ALU.add))
            self.turn(t1, y)
            self.turn(t2, z)
            self.linear_t(t3, [(w1[:], t1), (w2[:], t2)], b[:])
            self.turn(y, t3)

        @self.dve_steps
        def _(link):
            link(v.scalar_tensor_tensor(out=y[:], in0=y[:], scalar=0.2, in1=y[:], op0=ALU.mult, op1=ALU.max))
            link(v.tensor_tensor(z[:], y[:], y[:], ALU.mult))
            link(v.tensor_reduce(st[:, 0, :], view(z), AX_X, ALU.add))
        with nc.Block() as block:
            @block.scalar
            def _(sc):
                nc.scalar.activation(st[:, 1, :], st[:, 0, :], ACT.Sqrt)

        @self.dve_steps
        def _(link):
            link(v.tensor_scalar(st[:, 1, :], st[:, 1, :], 1e-12, None, ALU.max))
            link(v.reciprocal(st[:, 2, :], st[:, 1, :]))
            link(v.tensor_tensor(view(y), view(y), st[:, 2, :].unsqueeze(2).to_broadcast([P, NT, D]), ALU.mult))
            link(v.tensor_tensor(x[:], x[:], y[:], ALU.add))
        self.layer_norm(x, x, 1e-5)

    def attention_buffers(self):
        sb = self.sb
        self.u3 = sb("u3", [P, 3, HEADS, NT], BF16)
        self.v3 = sb("v3", [P, NT * 3 * 2 * HEADS], BF16)
        self.v_rank = sb("v_rank", [P, NT, 2 * HEADS])
        self.rest = sb("rest", [P, NT * 2 * HEADS])
        self.carry_row = sb("carry_row", [HEADS, 2, P + 1])
        self.carry = sb("carry", [P, 2, HEADS])
        self.att = sb("att", [P, 2 * HEADS])
        self.v_table = self.dram("v_table", [NP, 2 * HEADS])
        self.uv = sb("uv", [P, NT, 2 * HEADS])
        self.u_n = sb("u_n", [P, HEADS, NT])
        self.v_n = sb("v_n", [P, NT, 2 * HEADS])

    def layer_of_attention(self):
        a, v, y, z, view = self.a, self.nc.vector, self.y, self.z, rows_view
        uv, u_n, v_n = self.uv, self.u_n, self.v_n
        rounds = a["L2_gnn_W0"].shape[0]
        w1, w2 = (self.sb(n, [P, rounds, D]) for n in ("w1", "w2"))
        att, dist = self.sb("att", [P, rounds, 2]), self.sb("dist", [P, rounds, 3])
        self.load([pair for r in range(rounds) for pair in (
            (w1[:, r, :], a["L2_gnn_W1"][r]), (w2[:, r, :], a["L2_gnn_W2"][r]),
            (att[:, r, 0:1], a["L2_gnn_Wa"][r, 0:D, :]), (att[:, r, 1:2], a["L2_gnn_Wa"][r, D:2 * D, :]),
            (dist[:, r, 0:1], a["L2_gnn_W0"][r].to_broadcast([P, 1])),
            (dist[:, r, 1:2], a["L2_gnn_Wa"][r, 2 * D:, :].to_broadcast([P, 1])))])

        @self.dve_steps
        def _(link):
            link(v.memset(v_n[:], 0.0))
            link(v.tensor_tensor(dist[:, :, 2], dist[:, :, 0], dist[:, :, 1], ALU.mult))

        for r in range(rounds):
            with self.scope():
                t1, t2 = self.nodes("t1", "t2")
                self.turn(t1, z)
                self.linear_t(t2, [(w1[:, r, :], t1)])

                def spread(link):
                    link(v.tensor_copy(u_n[:, 0:1, :], uv[:, :, 0:1].rearrange("p i k -> p k i")))
                    link(v.tensor_copy(v_n[:, :, 0:1], uv[:, :, 1:2]))

                self.project(t1, t2, w1[:, r, :], att[:, r, :], 2, spread, w2[:, r, :])
            with self.scope():
                ahead = 68
                self.lg_a = self.sb("lg_a", [P, 1, TILES])
                self.edge_logits(u_n[:, 0:1, :], 1, 1, self.table, ahead)
                self.segment_softmax(1, 0.01, dist=dist[:, r, 2:3])
                self.sum_pass(self.table, self.lg_a, ahead=ahead)
            with self.scope():
                agg = self.sb("agg", [P, NT, D])
                self.to_nodes(self.agg, agg[:])

                @self.dve_steps
                def _(link):
                    link(v.tensor_tensor(view(z), view(z), agg[:], ALU.add))
                    link(v.tensor_scalar(z[:], z[:], 0.0, None, ALU.max))

        kept = self.kept.rearrange("(i p) f -> p i f", p=P)
        self.load([(view(y), kept)])

        @self.dve_steps
        def _(link):
            link(v.tensor_tensor(z[:], y[:], z[:], ALU.add))
        self.layer_norm(z, z, 1e-5)
        self.load([(kept, view(z))])

    def layer_of_heads(self):
        a, v, y, z, view, att = self.a, self.nc.vector, self.y, self.z, rows_view, self.att
        uv, u_n, v_n = self.uv, self.u_n, self.v_n
        gamma, beta, bias = self.matrices("gamma", "beta", "bias")
        share = self.sb("share", [P, NT, HEADS])
        with self.scope():
            t1, t2 = self.nodes("t1", "t2")
            w, = self.matrices("w")

            @self.dve_steps
            def _(link):
                link(v.memset(att[:], 0.0))
            with self.nc.allow_non_contiguous_dma(reason="256 attention weights as columns"):
                self.load([(w[:], a["L3_gnn_W"]), (gamma[:], on_all(a["L3_gnn_gamma"])), (beta[:], on_all(a["L3_gnn_beta"])),
                           (bias[:], on_all(a["L3_gnn_bias"]))]
                          + [(att[h * HD:(h + 1) * HD, s * HEADS + h:s * HEADS + h + 1], column(a[n][0, h]))
                             for s, n in enumerate(("L3_gnn_att_src", "L3_gnn_att_dst")) for h in range(HEADS)])
            self.turn(t1, z)
            self.linear_t(t2, [(w[:], t1)])

            def spread(link):
                link(v.tensor_copy(u_n[:], uv[:, :, 0:HEADS].rearrange("p i k -> p k i")))
                link(v.tensor_copy(v_n[:, :, 0:HEADS], uv[:, :, HEADS:]))
                link(v.tensor_tensor(v_n[:, :, HEADS:], uv[:, :, 0:HEADS], uv[:, :, HEADS:], ALU.add))

            self.project(t1, t2, w[:], att[:], 2 * HEADS, spread)
        with self.scope():
            ahead = AHEAD
            self.own_d = self.dram("own_d", [EP, HEADS])
            self.lg_a = self.sb("lg_a", [P, HEADS, TILES])
            self.self_a = self.sb("self_a", [P, HEADS, TILES])
            self.edge_logits(u_n[:], HEADS, 2 * HEADS, self.table, ahead)
            self.segment_softmax(HEADS, 0.2, own=True)
            self.sum_pass(self.table, self.lg_a, heads=True, ahead=ahead, shares=(self.own_d, share[:]))
        with self.scope():
            agg = self.sb("agg", [P, NT, D + HEADS])
            self.to_nodes(self.agg3, agg[:], share[:])

            @self.dve_steps
            def _(link):
                for h in range(HEADS):
                    link(v.tensor_tensor(view(y)[:, :, h * HD:(h + 1) * HD], view(y)[:, :, h * HD:(h + 1) * HD],
                                        agg[:, :, D + h:D + h + 1].to_broadcast([P, NT, HD]), ALU.mult))
                link(v.tensor_tensor(view(y), view(y), agg[:, :, 0:D], ALU.add))
                link(v.tensor_tensor(view(y), view(y), bias[:].unsqueeze(1).to_broadcast([P, NT, D]), ALU.add))
        self.layer_norm(y, y, 1e-5, gamma, beta)

        @self.dve_steps
        def _(link):
            link(v.tensor_scalar(y[:], y[:], 0.0, None, ALU.max))
            link(v.tensor_tensor(z[:], z[:], y[:], ALU.add))
        self.layer_norm(z, z, 1e-5)


def graph_layers(nc, args, out):
    with ExitStack() as ctx:
        Kernel(nc, ctx, args, out).run()


def kernel(**inputs):
    import concourse.bacc as bacc
    from concourse.bass_utils import run_bass_kernel_spmd

    nc = bacc.Bacc("TRN2", target_bir_lowering=False, num_devices=1)
    arrays, args = {}, {}
    for name, value in inputs.items():
        value = np.ascontiguousarray(value)
        arrays[f"in_{name}"] = value
        args[name] = nc.dram_tensor(f"in_{name}", value.shape, mybir.dt.from_np(value.dtype), kind="ExternalInput").ap()
    out = nc.dram_tensor("out_x", (N, D), F32, kind="ExternalOutput").ap()
    graph_layers(nc, args, out)
    result = run_bass_kernel_spmd(nc, [arrays], core_ids=[0])
    return result.results[0]["out_x"]
```
